# Optimizing a Trainium2 kernel written in Bass

```python
import numpy as np
import jax
import jax.numpy as jnp

def _softmax(x, axis=-1):
    return jax.nn.softmax(x, axis=axis)

def _gelu(x):
    return jax.nn.gelu(x, approximate=True)

def _silu(x):
    return jax.nn.silu(x)

def _sigmoid(x):
    return jax.nn.sigmoid(x)

def _layernorm(x, axis=-1, eps=1e-05):
    m = jnp.mean(x, axis=axis, keepdims=True)
    v = jnp.var(x, axis=axis, keepdims=True)
    return (x - m) / jnp.sqrt(v + eps)

def _scatter_add(tgt, idx, src, axis=0):
    return tgt.at[idx].add(src)

def _segment_sum(src, seg, n):
    return jax.ops.segment_sum(src, seg, n)
kernel_name = 'mk_cond_seq_d2_seqx_r8_09370b'

def setup_inputs(seed: int=0):
    np.random.seed(seed)
    _w = jnp.asarray

    def _rec_inputs():
        import jax
        import jax.numpy as jnp
        _rk = jax.random.key(seed)
        x = -0.0002928 + 1 * jax.random.normal(jax.random.fold_in(_rk, 1), (64, 32, 128), jnp.float32)
        _lenS = 32 - jax.random.randint(jax.random.fold_in(_rk, 7), (64,), 0, max(1, 32 // 4) + 1, jnp.int32)
        _lenS2 = 32 - jax.random.randint(jax.random.fold_in(_rk, 8), (64,), 0, max(1, 32 // 4) + 1, jnp.int32)
        itok_B_0_7 = jax.random.randint(jax.random.fold_in(_rk, 11), (64,), 0, 8, jnp.int32)
        itok_B_6_14 = jax.random.randint(jax.random.fold_in(_rk, 12), (64,), 6, 15, jnp.int32)
        return (x, itok_B_0_7, itok_B_6_14)
    x, itok_B_0_7, itok_B_6_14 = _rec_inputs()

    def _L0_cond_setup():
        import jax, jax.numpy as jnp
        import numpy as np
        E, H, I = (8, 128, 512)
        B, S = (4, 128)
        LN_EPS = 1e-12
        key = jax.random.key(seed)
        ks = jax.random.split(key, 8)
        x = jax.random.normal(ks[0], (B, S, H), dtype=jnp.float32)
        expert_idx = jax.random.randint(ks[1], (B,), 0, E, dtype=jnp.int64)
        Wi = jax.random.normal(ks[2], (E, H, I), dtype=jnp.float32) * 0.02
        bi = jnp.zeros((E, I), dtype=jnp.float32)
        Wo = jax.random.normal(ks[3], (E, I, H), dtype=jnp.float32) * 0.02
        bo = jnp.zeros((E, H), dtype=jnp.float32)
        gamma = jnp.ones((E, H), dtype=jnp.float32)
        beta = jnp.zeros((E, H), dtype=jnp.float32)
        return {'input_tensor': x, 'expert_idx': expert_idx, 'Wi': Wi, 'bi': bi, 'Wo': Wo, 'bo': bo, 'gamma': gamma, 'beta': beta}
    _L0_cond_all = _L0_cond_setup()
    _L0_cond_in = {k: v for k, v in _L0_cond_all.items() if k in ('Wi', 'bi', 'Wo', 'bo', 'gamma', 'beta')}
    del _L0_cond_all

    def _L1_cond_setup():
        import jax, jax.numpy as jnp
        import numpy as np
        D = 128
        E = 8
        FF = 512
        TOPK = 2
        S = 32
        SE = 64
        SH = 128
        B, T = (2, 256)

        def _forward(x, subject_ids, ln_g, ln_b, subj_emb, hyp_w1, hyp_b1, hyp_w2, hyp_b2, sty_w1, sty_b1, sty_w2, sty_b2, router_w, exp_w1, exp_b1, exp_w2, exp_b2):
            mu = x.mean(-1, keepdims=True)
            var = x.var(-1, keepdims=True)
            h = (x - mu) * jax.lax.rsqrt(var + 1e-05) * ln_g + ln_b
            m_t = h.mean(1, keepdims=True)
            v_t = h.var(1, keepdims=True)
            h_norm = (h - m_t) * jax.lax.rsqrt(v_t + 1e-08)
            se = subj_emb[subject_ids]
            hyp = jax.nn.relu(se @ hyp_w1 + hyp_b1) @ hyp_w2 + hyp_b2
            sty = jax.nn.relu(hyp @ sty_w1 + sty_b1) @ sty_w2 + sty_b2
            gamma, beta = jnp.split(sty, 2, axis=-1)
            gamma = jax.nn.softplus(gamma) + 1e-08
            h = h_norm * gamma[:, None, :] + beta[:, None, :]
            h_flat = h.reshape(-1, D)
            probs = jax.nn.softmax(h_flat @ router_w, axis=-1)
            gates, idx = jax.lax.top_k(probs, TOPK)
            gates = gates / gates.sum(-1, keepdims=True)
            N = h_flat.shape[0]
            combine = jnp.zeros((N, E), h_flat.dtype).at[jnp.arange(N)[:, None], idx].add(gates)
            hid = jax.nn.relu(jnp.einsum('nd,edf->nef', h_flat, exp_w1) + exp_b1)
            eout = jnp.einsum('nef,efd->ned', hid, exp_w2) + exp_b2
            y = jnp.einsum('ned,ne->nd', eout, combine)
            return x + y.reshape(x.shape)
        key = jax.random.key(seed)
        ks = jax.random.split(key, 16)
        n = lambda k, sh, s=0.02: jax.random.normal(k, sh, dtype=jnp.float32) * s
        return {'x': jax.random.normal(ks[0], (B, T, D), dtype=jnp.float32), 'subject_ids': jax.random.randint(ks[1], (B,), 0, S), 'ln_g': jnp.ones((D,), jnp.float32), 'ln_b': jnp.zeros((D,), jnp.float32), 'subj_emb': n(ks[2], (S, SE)), 'hyp_w1': n(ks[3], (SE, SH), 1.0 / np.sqrt(SE)), 'hyp_b1': jnp.zeros((SH,), jnp.float32), 'hyp_w2': n(ks[4], (SH, SH), 1.0 / np.sqrt(SH)), 'hyp_b2': jnp.zeros((SH,), jnp.float32), 'sty_w1': n(ks[5], (SH, SH // 2), 1.0 / np.sqrt(SH)), 'sty_b1': jnp.zeros((SH // 2,), jnp.float32), 'sty_w2': n(ks[6], (SH // 2, 2 * D), 1.0 / np.sqrt(SH // 2)), 'sty_b2': jnp.zeros((2 * D,), jnp.float32), 'router_w': n(ks[7], (D, E), 1.0 / np.sqrt(D)), 'exp_w1': n(ks[8], (E, D, FF), 1.0 / np.sqrt(D)), 'exp_b1': jnp.zeros((E, FF), jnp.float32), 'exp_w2': n(ks[9], (E, FF, D), 1.0 / np.sqrt(FF)), 'exp_b2': jnp.zeros((E, D), jnp.float32)}
    _L1_cond_all = _L1_cond_setup()
    _L1_cond_in = {k: v for k, v in _L1_cond_all.items() if k in ('ln_g', 'ln_b', 'subj_emb', 'hyp_w1', 'hyp_b1', 'hyp_w2', 'hyp_b2', 'sty_w1', 'sty_b1', 'sty_w2', 'sty_b2', 'router_w', 'exp_w1', 'exp_b1', 'exp_w2', 'exp_b2')}
    del _L1_cond_all
    return {'x': x, 'itok_B_0_7': itok_B_0_7, 'itok_B_6_14': itok_B_6_14, 'L0_cond_Wi': _L0_cond_in['Wi'], 'L0_cond_bi': _L0_cond_in['bi'], 'L0_cond_Wo': _L0_cond_in['Wo'], 'L0_cond_bo': _L0_cond_in['bo'], 'L0_cond_gamma': _L0_cond_in['gamma'], 'L0_cond_beta': _L0_cond_in['beta'], 'L1_cond_ln_g': _L1_cond_in['ln_g'], 'L1_cond_ln_b': _L1_cond_in['ln_b'], 'L1_cond_subj_emb': _L1_cond_in['subj_emb'], 'L1_cond_hyp_w1': _L1_cond_in['hyp_w1'], 'L1_cond_hyp_b1': _L1_cond_in['hyp_b1'], 'L1_cond_hyp_w2': _L1_cond_in['hyp_w2'], 'L1_cond_hyp_b2': _L1_cond_in['hyp_b2'], 'L1_cond_sty_w1': _L1_cond_in['sty_w1'], 'L1_cond_sty_b1': _L1_cond_in['sty_b1'], 'L1_cond_sty_w2': _L1_cond_in['sty_w2'], 'L1_cond_sty_b2': _L1_cond_in['sty_b2'], 'L1_cond_router_w': _L1_cond_in['router_w'], 'L1_cond_exp_w1': _L1_cond_in['exp_w1'], 'L1_cond_exp_b1': _L1_cond_in['exp_b1'], 'L1_cond_exp_w2': _L1_cond_in['exp_w2'], 'L1_cond_exp_b2': _L1_cond_in['exp_b2']}

def reference(x, itok_B_0_7, itok_B_6_14, L0_cond_Wi, L0_cond_bi, L0_cond_Wo, L0_cond_bo, L0_cond_gamma, L0_cond_beta, L1_cond_ln_g, L1_cond_ln_b, L1_cond_subj_emb, L1_cond_hyp_w1, L1_cond_hyp_b1, L1_cond_hyp_w2, L1_cond_hyp_b2, L1_cond_sty_w1, L1_cond_sty_b1, L1_cond_sty_w2, L1_cond_sty_b2, L1_cond_router_w, L1_cond_exp_w1, L1_cond_exp_b1, L1_cond_exp_w2, L1_cond_exp_b2):
    import jax
    import jax.numpy as jnp

    def _L0_cond_ref(input_tensor, expert_idx, Wi, bi, Wo, bo, gamma, beta):
        import jax, jax.numpy as jnp
        import numpy as np
        E, H, I = (8, 128, 512)
        B, S = (4, 128)
        LN_EPS = 1e-12
        Wi_b = Wi[expert_idx]
        bi_b = bi[expert_idx]
        Wo_b = Wo[expert_idx]
        bo_b = bo[expert_idx]
        g_b = gamma[expert_idx]
        be_b = beta[expert_idx]
        h = jax.nn.gelu(jnp.einsum('bsh,bhi->bsi', input_tensor, Wi_b) + bi_b[:, None, :], approximate=False)
        o = jnp.einsum('bsi,bih->bsh', h, Wo_b) + bo_b[:, None, :]
        r = o + input_tensor
        mu = jnp.mean(r, axis=-1, keepdims=True)
        var = jnp.mean(jnp.square(r - mu), axis=-1, keepdims=True)
        y = (r - mu) * jax.lax.rsqrt(var + LN_EPS)
        return y * g_b[:, None, :] + be_b[:, None, :]

    def _L1_cond_ref(x, subject_ids, ln_g, ln_b, subj_emb, hyp_w1, hyp_b1, hyp_w2, hyp_b2, sty_w1, sty_b1, sty_w2, sty_b2, router_w, exp_w1, exp_b1, exp_w2, exp_b2):
        import jax, jax.numpy as jnp
        import numpy as np
        D = 128
        E = 8
        FF = 512
        TOPK = 2
        S = 32
        SE = 64
        SH = 128
        B, T = (2, 256)

        def _forward(x, subject_ids, ln_g, ln_b, subj_emb, hyp_w1, hyp_b1, hyp_w2, hyp_b2, sty_w1, sty_b1, sty_w2, sty_b2, router_w, exp_w1, exp_b1, exp_w2, exp_b2):
            mu = x.mean(-1, keepdims=True)
            var = x.var(-1, keepdims=True)
            h = (x - mu) * jax.lax.rsqrt(var + 1e-05) * ln_g + ln_b
            m_t = h.mean(1, keepdims=True)
            v_t = h.var(1, keepdims=True)
            h_norm = (h - m_t) * jax.lax.rsqrt(v_t + 1e-08)
            se = subj_emb[subject_ids]
            hyp = jax.nn.relu(se @ hyp_w1 + hyp_b1) @ hyp_w2 + hyp_b2
            sty = jax.nn.relu(hyp @ sty_w1 + sty_b1) @ sty_w2 + sty_b2
            gamma, beta = jnp.split(sty, 2, axis=-1)
            gamma = jax.nn.softplus(gamma) + 1e-08
            h = h_norm * gamma[:, None, :] + beta[:, None, :]
            h_flat = h.reshape(-1, D)
            probs = jax.nn.softmax(h_flat @ router_w, axis=-1)
            gates, idx = jax.lax.top_k(probs, TOPK)
            gates = gates / gates.sum(-1, keepdims=True)
            N = h_flat.shape[0]
            combine = jnp.zeros((N, E), h_flat.dtype).at[jnp.arange(N)[:, None], idx].add(gates)
            hid = jax.nn.relu(jnp.einsum('nd,edf->nef', h_flat, exp_w1) + exp_b1)
            eout = jnp.einsum('nef,efd->ned', hid, exp_w2) + exp_b2
            y = jnp.einsum('ned,ne->nd', eout, combine)
            return x + y.reshape(x.shape)
        return _forward(x, subject_ids, ln_g, ln_b, subj_emb, hyp_w1, hyp_b1, hyp_w2, hyp_b2, sty_w1, sty_b1, sty_w2, sty_b2, router_w, exp_w1, exp_b1, exp_w2, exp_b2)
    x = _L0_cond_ref(x, itok_B_0_7, L0_cond_Wi, L0_cond_bi, L0_cond_Wo, L0_cond_bo, L0_cond_gamma, L0_cond_beta)
    x = _L1_cond_ref(x, itok_B_6_14, L1_cond_ln_g, L1_cond_ln_b, L1_cond_subj_emb, L1_cond_hyp_w1, L1_cond_hyp_b1, L1_cond_hyp_w2, L1_cond_hyp_b2, L1_cond_sty_w1, L1_cond_sty_b1, L1_cond_sty_w2, L1_cond_sty_b2, L1_cond_router_w, L1_cond_exp_w1, L1_cond_exp_b1, L1_cond_exp_w2, L1_cond_exp_b2)
    return x

_drawn_inputs = setup_inputs


def setup_inputs(seed=0):
    import zlib

    import numpy as np

    out = dict(_drawn_inputs(seed))
    spreads = {'L0_cond_bi': (0.0, 0.1),
     'L0_cond_bo': (0.0, 0.1),
     'L0_cond_gamma': (1.0, 0.2),
     'L0_cond_beta': (0.0, 0.1),
     'L1_cond_ln_g': (1.0, 0.2),
     'L1_cond_ln_b': (0.0, 0.1),
     'L1_cond_hyp_b1': (0.0, 0.1),
     'L1_cond_hyp_b2': (0.0, 0.1),
     'L1_cond_sty_b1': (0.0, 0.1),
     'L1_cond_sty_b2': (0.0, 0.1),
     'L1_cond_exp_b1': (0.0, 0.1),
     'L1_cond_exp_b2': (0.0, 0.1)}
    factors = {}
    for name, (base, spread) in spreads.items():
        noise = np.random.default_rng([zlib.crc32(name.encode()), seed]).standard_normal(out[name].shape)
        drawn = base * np.exp(spread * noise) if base else spread * noise
        out[name] = jnp.asarray(drawn.astype(out[name].dtype))
    for name, factor in factors.items():
        out[name] = (out[name] * factor).astype(out[name].dtype)
    return out
```

```python
from contextlib import ExitStack

import concourse.bass as bass
from concourse import mybir

F32 = mybir.dt.float32
F32R = mybir.dt.float32r
I32 = mybir.dt.int32
ALU = mybir.AluOpType
ACT = mybir.ActivationFunctionType
AX = mybir.AxisListType

P = 128


class Chain:

    def __init__(self, engine, semaphore):
        self.engine, self.semaphore, self.count, self.extra = engine, semaphore, 0, 0

    def mark(self, instruction):
        self.count += 1
        instruction.then_inc(self.semaphore, 1)

    def link(self, instruction):
        self.mark(instruction)
        self.engine.wait_ge(self.semaphore, self.count + self.extra)

    def enter(self, i, per_turn):
        self.start, self.per_turn, self.extra = self.count, per_turn, i * per_turn

    def leave(self, turns):
        assert self.count - self.start == self.per_turn, (self.count - self.start, self.per_turn)
        self.count, self.extra = self.start + turns * self.per_turn, 0


def build(nc, x, expert_of, subject_of, Wi, bi, Wo, bo, gamma, beta, ln_g, ln_b, subj_emb, hyp_w1, hyp_b1,
          hyp_w2, hyp_b2, sty_w1, sty_b1, sty_w2, sty_b2, router_w, exp_w1, exp_b1, exp_w2, exp_b2, out):
    NS, S, D = x.shape
    E, _, FF = Wi.shape
    NU, SE = subj_emb.shape
    SH, SH2 = sty_w1.shape
    N = NS * S
    FT = FF // P
    TT = N // P
    SPT = P // S
    C = 512
    NB = N // C
    SB = C // S
    TB = C // P
    G = 8
    CW = G * S
    NW = (NS - E) // G + E
    assert D == P and NW % 2 == 1
    NP = N + CW

    x_rows = x.rearrange("s t d -> (s t) d")
    out_rows = out.rearrange("s t d -> (s t) d")
    gate_rows = nc.dram_tensor("gate_rows", [NB, E * C], F32, kind="Internal").ap()

    def col(v):
        return v.rearrange("(p o) -> p o", o=1)

    with ExitStack() as ctx:
        def sb(name, shape, dt=F32):
            return ctx.enter_context(nc.sbuf_tensor(name, shape, dt))

        def sem(name):
            return ctx.enter_context(nc.semaphore(name))

        bank = [ctx.enter_context(nc.psum_tensor(f"bank{i}", [P, 512], F32)) for i in range(8)]

        ident = sb("ident", [P, P])
        iota_row = sb("iota_row", [P, NS])
        iota_part = sb("iota_part", [P, 1])
        iota_diag = sb("iota_diag", [P, P])
        part_of_quarter = sb("part_of_quarter", [NS, SPT, P])
        eps = sb("eps", [P, 2])
        zero_cols = sb("zero_cols", [P, CW])

        ids_all = sb("ids_all", [P, NS], I32)
        ids_col = sb("ids_col", [NS, 2], I32)
        key_all = sb("key_all", [P, NS])
        key_col = sb("key_col", [NS, 1])
        idf_all = sb("idf_all", [P, NS])
        idf_col = sb("idf_col", [NS, 2])
        smaller = sb("smaller", [NS, NS])
        place = sb("place", [NS, 1])
        perm = sb("perm", [NS, NS])
        below = sb("below", [P, E + 1, NS])
        first_of = sb("first_of", [P, E + 1])
        number = sb("number", [P, E])
        steps_cmp = sb("steps_cmp", [P, E, G])
        windows = sb("windows", [P, E])
        upto_mask = sb("upto_mask", [P, E, E])
        upto_part = sb("upto_part", [P, E, E])
        windows_in = sb("windows_in", [P, E])
        base_val = sb("base_val", [P, E])
        win_cmp = sb("win_cmp", [P, NW, E])
        win_expert = sb("win_expert", [P, NW])
        win_hot = sb("win_hot", [P, NW, E])
        win_part = sb("win_part", [P, NW, E])
        win_start = sb("win_start", [P, NW])
        table = sb("table", [1, 2, NW], I32)
        hot_expert = sb("hot_expert", [NS, E])
        hot_subject = sb("hot_subject", [NS, NU])
        win_hot_t = sb("win_hot_t", [E, NW])
        row_index = sb("row_index", [P, TT], I32)
        part_in_sample = sb("part_in_sample", [P, 1])
        sorted_expert = sb("sorted_expert", [E, NS])
        sorted_subject = sb("sorted_subject", [NU, NS])

        bi_r = sb("bi_r", [E, FF])
        b1_r = sb("b1_r", [E, FF])
        b2_r = sb("b2_r", [E, D])
        gbb_r = sb("gbb_r", [E, 3, D])
        cols = sb("cols", [P, 7])
        HB1, HB2, SB1, SG, SBT, LG, LB = range(7)
        emb = sb("emb", [NU, SE])
        hw1 = sb("hw1", [SE, SH])
        hw2 = sb("hw2", [SH, SH])
        sw1 = sb("sw1", [SH, SH2])
        sw2 = sb("sw2", [SH2, 2 * D])
        rw = sb("rw", [D, E])
        per_sample = sb("per_sample", [P, 3, NS])
        bi_c = sb("bi_c", [P, FT, NW])
        b1_c = sb("b1_c", [P, FT, E])
        se_t = sb("se_t", [SE, NS])
        hyp_t = sb("hyp_t", [SH, NS])
        hyp2_t = sb("hyp2_t", [SH, NS])
        sty_t = sb("sty_t", [SH2, NS])
        film_a = sb("film_a", [P, NS])
        film_b = sb("film_b", [P, NS])
        soft = sb("soft", [P, 3, NS])

        early = sb("early", [P, TT * D + NP])
        xg = early[:, 0:TT * D].rearrange("p (t d) -> p t d", d=D)
        xh = sb("xh", [P, NP], F32R)
        xl = sb("xl", [P, NP], F32R)
        xb = early[:, TT * D:]
        res = sb("res", [P, NP])
        wraw = sb("wraw", [P, 2, 2 * FF])
        wh = sb("wh", [P, 2, 2 * FF], F32R)
        wl = sb("wl", [P, 2, 2 * FF], F32R)
        act_f = sb("act_f", [P, 4, C])
        act_h = sb("act_h", [P, 4, C], F32R)
        act_l = sb("act_l", [P, 4, C], F32R)

        vraw = wraw
        vh = sb("vh", [P, E, 2 * FF], F32R)
        vl = sb("vl", [P, E, 2 * FF], F32R)
        t0 = sb("t0", [P, C])
        t1 = sb("t1", [P, C])
        sq = sb("sq", [P, C])
        y = sb("y", [P, C])
        hf = sb("hf", [P, C])
        hh, hl = xh, xl
        stats = sb("stats", [P, TB, 6])
        moments = sb("moments", [P, TB, 2])
        spread = sb("spread", [P, TB])
        normal = sb("normal", [P, TB, D])
        scratch = sb("scratch", [P, 1])
        carrier = sb("carrier", [P, 1])
        block_index = sb("block_index", [P, TB], I32)
        sums = sb("sums", [P, SB])
        rt = sb("rt", [P, SB])
        rmax = sb("rmax", [P, TB])
        rprob = sb("rprob", [P, TB, E])
        rs = sb("rs", [P, 6, TB, E])
        rv = sb("rv", [P, 6, TB])
        comb = sb("comb", [P, TB, E])
        comb_t = sb("comb_t", [E, C])
        gates = early[:, 0:E * C].rearrange("p (e c) -> p e c", e=E)
        weighted = sb("weighted", [P, 2, C])
        total = sb("total", [P, C])
        out_sb = sb("out_sb", [P, TB, D])

        names = """ids params consts consts2 consts3 idx_mm idx_ready perm_ready table_ready dve_own act_own pool_own
            small_mm small_out style_mm style_out x_turned x_high x_ready pads
            wi_high wo_high wi_low wo_low hid_mm gelu_done split_done out_mm win_done v_high v_low
            res_turned var1_ready sd1_ready normed1 back1 scaled1 y_ready y_turned var2_ready sd2_ready normed2 back2
            affine time_centred time_squared time_var time_sd fetched film_ready pool_film film_done h_high h_low
            logits_mm rmax_done exp_done comb_ready comb_mm comb_copied gates_stored bias_mm total_init
            up_mm relu_done relu_high relu_high_v relu_low down_mm weighted_done added out_turned out_copied
            index_copied stored"""
        s = {name: sem(name) for name in names.split()}
        gathered = [sem(f"gathered{j}") for j in range(NB)]
        wi_landed = [sem("wi_landed0"), sem("wi_landed1")]
        wo_landed = [sem("wo_landed0"), sem("wo_landed1")]
        gates_loaded = [sem("gates_loaded0"), sem("gates_loaded1")]
        v_landed = [sem("v_landed0"), sem("v_landed1")]
        block = ctx.enter_context(nc.Block())

        L = E * FT
        FIRST = 3
        up_bank = [bank[0], bank[1], bank[2]]
        down_bank = [bank[4], bank[5]]

        @block.sync
        def _(sp):
            sp.dma_start(ids_all[:], expert_of.partition_broadcast(P)).then_inc(s["ids"], 16)
            sp.dma_start(ids_col[:, 0:1], col(expert_of)).then_inc(s["ids"], 16)
            sp.dma_start(ids_col[:, 1:2], col(subject_of)).then_inc(s["ids"], 16)
            for dst, src in ((bi_r[:], bi), (gbb_r[:, 0, :], gamma), (gbb_r[:, 1, :], beta), (gbb_r[:, 2, :], bo),
                             (b1_r[:], exp_b1), (b2_r[:], exp_b2), (emb[:], subj_emb), (hw1[:], hyp_w1),
                             (hw2[:], hyp_w2), (sw1[:], sty_w1), (sw2[:], sty_w2), (rw[:], router_w),
                             (cols[:, HB1:HB1 + 1], col(hyp_b1)), (cols[:, HB2:HB2 + 1], col(hyp_b2)),
                             (cols[0:SH2, SB1:SB1 + 1], col(sty_b1)), (cols[:, SG:SG + 1], col(sty_b2[0:D])),
                             (cols[:, SBT:SBT + 1], col(sty_b2[D:2 * D])), (cols[:, LG:LG + 1], col(ln_g)),
                             (cols[:, LB:LB + 1], col(ln_b))):
                sp.dma_start(dst, src).then_inc(s["params"], 16)
            sp.wait_ge(s["table_ready"], 1)

            def load(k, par, again):
                if again:
                    sp.wait_ge(s["wi_high"], k - 1)
                    sp.wait_ge(s["wi_low"], k - 1)
                e = sp.value_load(table[0:1, 0, bass.ds(k, 1)], min_val=0, max_val=E - 1)
                sp.dma_start(wraw[:, par, 0:FF], Wi[bass.ds(e, 1), :, :].rearrange("o p f -> p (o f)"))\
                    .then_inc(wi_landed[par], 16)
                if again:
                    sp.wait_ge(s["wo_high"], k - 1)
                    sp.wait_ge(s["wo_low"], k - 1)
                sp.dma_start(wraw[:, par, FF:2 * FF].rearrange("p (t d) -> p t d", t=FT),
                             Wo[bass.ds(e, 1), :, :].rearrange("o (t p) d -> p (o t) d", p=P))\
                    .then_inc(wo_landed[par], 16)

            load(0, 0, False)
            load(1, 1, False)
            with sp.Fori(1, NW // 2) as i:
                load(2 * i, 0, True)
                load(2 * i + 1, 1, True)
            load(NW - 1, 0, True)

            def load_v(e):
                par = (e + 1) % 2
                if e < 2:
                    for name in ("wi_high", "wi_low", "wo_high", "wo_low"):
                        sp.wait_ge(s[name], NW - 1 + e)
                else:
                    sp.wait_ge(s["v_high"], e - 1)
                    sp.wait_ge(s["v_low"], e - 1)
                sp.dma_start(wraw[:, par, 0:FF], exp_w1[e]).then_inc(wi_landed[par], 16)
                sp.dma_start(wraw[:, par, FF:2 * FF].rearrange("p (t d) -> p t d", t=FT),
                             exp_w2[e].rearrange("(t p) d -> p t d", p=P)).then_inc(wo_landed[par], 16)

            def gates_trip(b):
                sp.wait_ge(s["comb_copied"], b + 1)
                sp.dma_start(gate_rows[b:b + 1, :].rearrange("o (e c) -> (o e) c", e=E), comb_t[:])\
                    .then_inc(s["gates_stored"], 16)
                sp.wait_ge(s["gates_stored"], 16 * (b + 1))
                for half in range(2):
                    if b:
                        sp.wait_ge(s["weighted_done"], E * (b - 1) + E // 2 * (half + 1))
                    w = E * C // 2
                    sp.dma_start(gates[:, half * E // 2:(half + 1) * E // 2, :].rearrange("p e c -> p (e c)"),
                                 gate_rows[b, half * w:(half + 1) * w].partition_broadcast(P))\
                        .then_inc(gates_loaded[half], 16)

            load_v(0)
            load_v(1)
            load_v(2)
            load_v(3)
            gates_trip(0)
            for e in range(4, E):
                load_v(e)
            for b in range(1, NB):
                gates_trip(b)

        @block.gpsimd
        def _(pool):
            own = Chain(pool, s["pool_own"])
            nc.gpsimd.iota(iota_row[:], pattern=[[1, NS]], base=0, channel_multiplier=0,
                           allow_small_or_imprecise_dtypes=True).then_inc(s["consts"], 1)
            nc.gpsimd.iota(iota_part[:], pattern=[[1, 1]], base=0, channel_multiplier=1,
                           allow_small_or_imprecise_dtypes=True).then_inc(s["consts"], 1)
            nc.gpsimd.iota(iota_diag[:], pattern=[[1, P]], base=0, channel_multiplier=-1,
                           allow_small_or_imprecise_dtypes=True).then_inc(s["consts"], 1)
            nc.gpsimd.iota(upto_mask[:], pattern=[[1, E], [-1, E]], base=0, channel_multiplier=0,
                           allow_small_or_imprecise_dtypes=True).then_inc(s["consts"], 1)
            own.link(nc.gpsimd.memset(part_of_quarter[:], 0.0))
            for q in range(SPT):
                own.link(nc.gpsimd.iota(part_of_quarter[:, q, q * S:(q + 1) * S], pattern=[[0, S]], base=0,
                                        channel_multiplier=S, allow_small_or_imprecise_dtypes=True))
                own.link(nc.gpsimd.iota(part_in_sample[q * S:(q + 1) * S, :], pattern=[[1, 1]], base=0,
                                        channel_multiplier=1, allow_small_or_imprecise_dtypes=True))
            nc.gpsimd.memset(scratch[:], 0.0).then_inc(s["consts2"], 1)
            nc.gpsimd.memset(eps[:, 0:1], 1e-12).then_inc(s["consts3"], 1)
            nc.gpsimd.memset(eps[:, 1:2], 1e-5).then_inc(s["consts3"], 1)
            own.link(nc.gpsimd.memset(zero_cols[:], 0.0))
            nc.gpsimd.tensor_copy(xh[:, N:NP], zero_cols[:]).then_inc(s["pads"], 1)
            nc.gpsimd.tensor_copy(xl[:, N:NP], zero_cols[:]).then_inc(s["pads"], 1)
            nc.gpsimd.tensor_copy(xb[:, N:NP], zero_cols[:]).then_inc(s["pads"], 1)

            def gather(j):
                for t in range(j * TB, (j + 1) * TB):
                    pool.indirect_dma_start(xg[:, t, :], None, x_rows,
                                            bass.IndirectOffsetOnAxis(row_index[:, t:t + 1], 0)).then_inc(gathered[j], 16)

            def low_out(k, par, again):
                if again:
                    pool.wait_ge(s["out_mm"], k - 1)
                pool.wait_ge(wo_landed[par], 8 * (k - par) + 16)
                pool.wait_ge(s["wo_high"], k + 1)
                nc.gpsimd.tensor_tensor(wl[:, par, FF:], wraw[:, par, FF:], wh[:, par, FF:], ALU.subtract)\
                    .then_inc(s["wo_low"], 1)

            pool.wait_ge(s["idx_ready"], 1)
            gather(0)
            gather(1)
            for i in range(FIRST):
                low_out(2 * i, 0, i > 0)
                low_out(2 * i + 1, 1, i > 0)
                if i + 2 < NB:
                    gather(i + 2)
            with pool.Fori(FIRST, NW // 2) as i:
                low_out(2 * i, 0, True)
                low_out(2 * i + 1, 1, True)
            low_out(NW - 1, 0, True)

            def low_v(e):
                pool.wait_ge(s["v_high"], e + 1)
                nc.gpsimd.tensor_tensor(vl[:, e, :], wraw[:, (e + 1) % 2, :], vh[:, e, :], ALU.subtract)\
                    .then_inc(s["v_low"], 1)

            samples = lambda v: v.rearrange("p (a n) -> p a n", n=S)
            each = lambda v: v.unsqueeze(2).to_broadcast([P, SB, S])

            def add_beta(m):
                pool.wait_ge(s["scaled1"], m + 1)
                if not (isinstance(m, int) and m == 0):
                    pool.wait_ge(s["total_init"], m)
                nc.gpsimd.tensor_tensor(samples(y[:]), samples(t1[:]), each(per_sample[:, 1, bass.ds(m * SB, SB)]),
                                        ALU.add).then_inc(s["y_ready"], 1)

            def film(m):
                pool.wait_ge(s["film_ready"], m + 1)
                nc.gpsimd.tensor_tensor(samples(t1[:]), samples(t1[:]), each(rt[:]), ALU.mult).then_inc(s["pool_film"], 1)
                pool.wait_ge(s["pool_film"], m + 1)
                nc.gpsimd.tensor_tensor(samples(hf[:]), samples(t1[:]), each(film_b[:, bass.ds(m * SB, SB)]), ALU.add)\
                    .then_inc(s["film_done"], 1)

            def low_tokens(m):
                pool.wait_ge(s["h_high"], m + 1)
                nc.gpsimd.tensor_tensor(hl[:, bass.ds(m * C, C)], hf[:], hh[:, bass.ds(m * C, C)], ALU.subtract)\
                    .then_inc(s["h_low"], 1)

            def add(b, e):
                pool.wait_ge(s["weighted_done"], E * b + e + 1)
                if e:
                    pool.wait_ge(s["added"], E * b + e)
                else:
                    pool.wait_ge(s["total_init"], b + 1)
                nc.gpsimd.tensor_tensor(total[:], total[:], weighted[:, e % 2, :], ALU.add).then_inc(s["added"], 1)

            def scatter(b):
                pool.wait_ge(s["out_copied"], b + 1)
                nc.gpsimd.tensor_copy(block_index[:], row_index[:, bass.ds(b * TB, TB)]).then_inc(s["index_copied"], 1)
                pool.wait_ge(s["index_copied"], b + 1)
                nc.gpsimd.tensor_tensor(scratch[:], scratch[:], scratch[:], ALU.add)
                for t in range(TB):
                    pool.indirect_dma_start(out_rows, bass.IndirectOffsetOnAxis(block_index[:, t:t + 1], 0),
                                            out_sb[:, t, :], None).then_inc(s["stored"], 16)

            def experts(b, first, last):
                if not first:
                    add(b - 1, E - 1)
                    scatter(b - 1)
                for e in range(E - 1):
                    if e == 1 and not last:
                        add_beta(b + 1)
                    if first and e + 2 < E:
                        low_v(e + 2)
                    add(b, e)
                    if e == 3 and not last:
                        film(b + 1)
                        low_tokens(b + 1)

            add_beta(0)
            low_v(0)
            film(0)
            low_tokens(0)
            low_v(1)
            experts(0, True, False)
            with pool.Fori(1, NB - 1) as b:
                experts(b, False, False)
            experts(NB - 1, False, True)
            add(NB - 1, E - 1)
            scatter(NB - 1)
            pool.wait_ge(s["stored"], 16 * TT)

        @block.vector
        def _(dve):
            own = Chain(dve, s["dve_own"])
            V = nc.vector

            dve.wait_ge(s["consts"], 4)
            dve.wait_ge(s["ids"], 48)
            own.mark(V.tensor_copy(idf_all[:], ids_all[:]))
            own.mark(V.tensor_scalar(ident[:], iota_diag[:], 0.0, None, ALU.is_equal))
            own.link(V.tensor_copy(idf_col[:], ids_col[:]))
            own.mark(V.scalar_tensor_tensor(key_all[:], idf_all[:], float(NS), iota_row[:], ALU.mult, ALU.add))
            own.link(V.scalar_tensor_tensor(key_col[:], idf_col[:, 0:1], float(NS), iota_part[0:NS, :], ALU.mult, ALU.add))
            own.link(V.tensor_scalar(smaller[:], key_all[0:NS, :], key_col[:, 0:1], None, ALU.is_lt))
            own.link(V.tensor_reduce(place[:], smaller[:], AX.X, ALU.add))
            V.tensor_scalar(perm[:], iota_row[0:NS, :], place[:, 0:1], None, ALU.is_equal).then_inc(s["perm_ready"], 1)

            dve.wait_ge(s["idx_mm"], 1)
            V.tensor_scalar(row_index[:], bank[0][:, 0:TT], part_in_sample[:, 0:1], None, ALU.add)\
                .then_inc(s["idx_ready"], 1)

            own.link(V.tensor_tensor(below[:], idf_all[:].unsqueeze(1).to_broadcast([P, E + 1, NS]),
                                     iota_row[:, 0:E + 1].unsqueeze(2).to_broadcast([P, E + 1, NS]), ALU.is_lt))
            own.link(V.tensor_reduce(first_of[:], below[:], AX.X, ALU.add))
            own.link(V.tensor_tensor(number[:], first_of[:, 1:E + 1], first_of[:, 0:E], ALU.subtract))
            steps = iota_row[:, 0:NS].rearrange("p (a g) -> p g a", g=G)[:, 0, 0:G]
            own.link(V.tensor_tensor(steps_cmp[:], number[:].unsqueeze(2).to_broadcast([P, E, G]),
                                     steps.unsqueeze(1).to_broadcast([P, E, G]), ALU.is_gt))
            own.link(V.tensor_reduce(windows[:], steps_cmp[:], AX.X, ALU.add))
            own.link(V.tensor_scalar(upto_part[:], upto_mask[:], 0.0, None, ALU.is_ge))
            own.link(V.tensor_tensor(upto_part[:], upto_part[:], windows[:].unsqueeze(1).to_broadcast([P, E, E]), ALU.mult))
            own.link(V.tensor_reduce(windows_in[:], upto_part[:], AX.X, ALU.add))
            own.link(V.tensor_tensor(base_val[:], windows_in[:], windows[:], ALU.subtract))
            own.link(V.scalar_tensor_tensor(base_val[:], base_val[:], -float(G), first_of[:, 0:E], ALU.mult, ALU.add))
            own.link(V.tensor_tensor(win_cmp[:], windows_in[:].unsqueeze(1).to_broadcast([P, NW, E]),
                                     iota_row[:, 0:NW].unsqueeze(2).to_broadcast([P, NW, E]), ALU.is_le))
            own.link(V.tensor_reduce(win_expert[:], win_cmp[:], AX.X, ALU.add))
            own.link(V.tensor_scalar(win_expert[:], win_expert[:], float(E - 1), None, ALU.min))
            own.mark(V.tensor_scalar(win_hot_t[:], win_expert[0:E, :], iota_part[0:E, 0:1], None, ALU.is_equal))
            own.link(V.tensor_tensor(win_hot[:], iota_row[:, 0:E].unsqueeze(1).to_broadcast([P, NW, E]),
                                     win_expert[:].unsqueeze(2).to_broadcast([P, NW, E]), ALU.is_equal))
            own.link(V.tensor_tensor(win_part[:], win_hot[:], base_val[:].unsqueeze(1).to_broadcast([P, NW, E]), ALU.mult))
            own.link(V.tensor_reduce(win_start[:], win_part[:], AX.X, ALU.add))
            own.link(V.scalar_tensor_tensor(win_start[:], iota_row[:, 0:NW], float(G), win_start[:], ALU.mult, ALU.add))
            own.link(V.tensor_scalar(win_start[:], win_start[:], float(NS), float(S), ALU.min, ALU.mult))
            own.link(V.tensor_copy(table[:, 0, :], win_expert[0:1, :]))
            V.tensor_copy(table[:, 1, :], win_start[0:1, :]).then_inc(s["table_ready"], 1)
            own.link(V.tensor_scalar(hot_expert[:], iota_row[0:NS, 0:E], idf_col[:, 0:1], None, ALU.is_equal))
            V.tensor_scalar(hot_subject[:], iota_row[0:NS, 0:NU], idf_col[:, 1:2], None, ALU.is_equal)\
                .then_inc(s["perm_ready"], 1)

            dve.wait_ge(s["small_mm"], 1)
            V.tensor_copy(sorted_expert[:], bank[1][0:E, 0:NS]).then_inc(s["small_out"], 1)
            V.tensor_copy(sorted_subject[:], bank[1][0:NU, NS:2 * NS]).then_inc(s["small_out"], 1)
            dve.wait_ge(s["small_mm"], 2)
            V.tensor_copy(per_sample[:], bank[2][:, 0:3 * NS].rearrange("p (a n) -> p a n", a=3)).then_inc(s["small_out"], 1)
            V.tensor_copy(bi_c[:], bank[3][:, 0:FT * NW].rearrange("p (a n) -> p a n", a=FT)).then_inc(s["small_out"], 1)
            V.tensor_copy(b1_c[:], bank[4][:, 0:FT * E].rearrange("p (a n) -> p a n", a=FT)).then_inc(s["small_out"], 1)

            dve.wait_ge(s["style_out"], 5)
            own.link(V.scalar_tensor_tensor(soft[:, 1, :], soft[:, 0, :], -1.0, soft[:, 0, :], ALU.mult, ALU.max))
            own.link(V.tensor_scalar(soft[:, 0, :], soft[:, 0, :], 0.0, None, ALU.max))
            V.tensor_scalar(soft[:, 2, :], soft[:, 1, :], -1.0, None, ALU.mult).then_inc(s["small_out"], 1)
            dve.wait_ge(s["style_out"], 6)
            own.link(V.tensor_tensor(film_a[:], soft[:, 0, :], soft[:, 1, :], ALU.add))
            own.link(V.tensor_scalar(film_a[:], film_a[:], 1e-8, None, ALU.add))

            def x_block(j):
                dve.wait_ge(s["x_high"], j + 1)
                bk = bank[6 + j % 2]
                V.tensor_tensor(xb[:, j * C:(j + 1) * C].rearrange("p (a n) -> p a n", n=S),
                                bk[:].rearrange("p (a n) -> p a n", n=S),
                                per_sample[:, 2, j * SB:(j + 1) * SB].unsqueeze(2).to_broadcast([P, SB, S]),
                                ALU.add).then_inc(s["x_ready"], 1)
                V.tensor_tensor(xl[:, j * C:(j + 1) * C], bk[:], xh[:, j * C:(j + 1) * C], ALU.subtract)\
                    .then_inc(s["x_ready"], 1)

            dve.wait_ge(s["small_out"], 5)
            x_block(0)

            def low_in(k, par, again):
                if again:
                    dve.wait_ge(s["hid_mm"], k - 1)
                dve.wait_ge(wi_landed[par], 8 * (k - par) + 16)
                dve.wait_ge(s["wi_high"], k + 1)
                V.tensor_tensor(wl[:, par, 0:FF], wraw[:, par, 0:FF], wh[:, par, 0:FF], ALU.subtract)\
                    .then_inc(s["wi_low"], 1)

            def split(k, par):
                dve.wait_ge(s["gelu_done"], 4 * (k + 1))
                a, h, l = (v[:, 2 * par:2 * par + 2, :] for v in (act_f, act_h, act_l))
                V.tensor_copy(h, a).then_inc(s["split_done"], 1)
                dve.wait_ge(s["split_done"], 2 * k + 1)
                V.tensor_tensor(l, a, h, ALU.subtract).then_inc(s["split_done"], 1)

            def finish(k, par):
                start = dve.value_load(table[0:1, 1, bass.ds(k, 1)], min_val=0, max_val=N)
                if not (isinstance(k, int) and k == 0):
                    dve.wait_ge(s["win_done"], k)
                dve.wait_ge(s["out_mm"], k + 1)
                V.tensor_tensor(res[:, bass.ds(start, CW)], down_bank[par][:, 0:CW], xb[:, bass.ds(start, CW)], ALU.add)\
                    .then_inc(s["win_done"], 1)

            def window(k, par, more, x_next=None):
                if par == 0 and x_next is not None:
                    x_block(x_next)
                split(k, par)
                if more:
                    low_in(k + 2, par, True)
                if not (isinstance(k, int) and k == 0):
                    finish(k - 1, 1 - par)

            dve.wait_ge(s["pads"], 3)
            low_in(0, 0, False)
            low_in(1, 1, False)
            for i in range(FIRST):
                window(2 * i, 0, True, i + 1 if i + 1 < NB else None)
                window(2 * i + 1, 1, True)
            with dve.Fori(FIRST, NW // 2 - 1) as i:
                window(2 * i, 0, True)
                window(2 * i + 1, 1, True)
            window(NW - 3, 0, True)
            window(NW - 2, 1, False)
            window(NW - 1, 0, False)
            finish(NW - 1, 0)

            samples = lambda v: v.rearrange("p (a n) -> p a n", n=S)
            each = lambda v: v.unsqueeze(2).to_broadcast([P, SB, S])
            tiles = lambda v: v.rearrange("p (t d) -> p t d", t=TB)
            perx = lambda v: v.unsqueeze(2).to_broadcast([P, TB, E])

            def moments_of(m, turned, ready):
                dve.wait_ge(s[turned], m + 1)
                for t in range(TB):
                    own.mark(V.bn_stats(stats[:, t, :], tiles(bank[6][:])[:, t, :]))
                dve.wait_ge(own.semaphore, own.count + own.extra)
                V.tensor_copy(carrier[:], iota_part[:])
                for t in range(TB):
                    own.mark(V.bn_aggr(moments[:, t, :], stats[:, t, :]))
                dve.wait_ge(own.semaphore, own.count + own.extra)
                eps = 1e-12 if ready == "var1_ready" else 1e-5
                V.tensor_scalar(spread[:], moments[:, :, 1], eps, None, ALU.add).then_inc(s[ready], 1)

            def normalise(m, sd, done):
                dve.wait_ge(s[sd], m + 1)
                own.link(V.reciprocal(spread[:], spread[:]))
                for t in range(TB):
                    ins = V.tensor_scalar(normal[:, t, :], tiles(bank[6][:])[:, t, :], moments[:, t, 0:1],
                                          spread[:, t:t + 1], ALU.subtract, ALU.mult)
                ins.then_inc(s[done], 1)

            def scale_gamma(m):
                dve.wait_ge(s["back1"], m + 1)
                V.tensor_tensor(samples(t1[:]), samples(bank[7][:]), each(per_sample[:, 0, bass.ds(m * SB, SB)]), ALU.mult)\
                    .then_inc(s["scaled1"], 1)

            def centre_time(m):
                dve.wait_ge(s["affine"], m + 1)
                own.link(V.tensor_reduce(sums[:], samples(t0[:]), AX.X, ALU.add))
                own.link(V.tensor_scalar(sums[:], sums[:], 1.0 / S, None, ALU.mult))
                V.tensor_tensor(samples(t1[:]), samples(t0[:]), each(sums[:]), ALU.subtract).then_inc(s["time_centred"], 1)

            def var_time(m):
                dve.wait_ge(s["time_squared"], m + 1)
                own.link(V.tensor_reduce(rt[:], samples(sq[:]), AX.X, ALU.add))
                V.tensor_scalar(rt[:], rt[:], 1.0 / S, 1e-8, ALU.mult, ALU.add).then_inc(s["time_var"], 1)

            def film_scale(m):
                dve.wait_ge(s["time_sd"], m + 1)
                own.link(V.reciprocal(rt[:], rt[:]))
                V.tensor_tensor(rt[:], rt[:], film_a[:, bass.ds(m * SB, SB)], ALU.mult).then_inc(s["film_ready"], 1)

            def router_max(m):
                logits = bank[6][:, 0:TB * E].rearrange("p (t e) -> p t e", e=E)
                dve.wait_ge(s["logits_mm"], m + 1)
                own.link(V.tensor_reduce(rmax[:], logits, AX.X, ALU.max))
                V.tensor_tensor(rprob[:], logits, perx(rmax[:]), ALU.subtract).then_inc(s["rmax_done"], 1)

            def router_pick(m):
                iota_e = iota_row[:, 0:E].unsqueeze(1).to_broadcast([P, TB, E])
                dve.wait_ge(s["exp_done"], m + 1)
                own.link(V.tensor_reduce(rv[:, 0, :], rprob[:], AX.X, ALU.add))
                own.link(V.reciprocal(rv[:, 1, :], rv[:, 0, :]))
                own.link(V.tensor_tensor(rprob[:], rprob[:], perx(rv[:, 1, :]), ALU.mult))
                own.link(V.tensor_reduce(rv[:, 2, :], rprob[:], AX.X, ALU.max))

                def pick(probs, largest, hot, number_):
                    own.link(V.tensor_tensor(hot, probs, perx(largest), ALU.is_equal))
                    own.link(V.scalar_tensor_tensor(hot, hot, -float(E), iota_e, ALU.mult, ALU.add))
                    own.link(V.tensor_reduce(number_, hot, AX.X, ALU.min))
                    own.link(V.tensor_tensor(hot, hot, perx(number_), ALU.is_equal))

                pick(rprob[:], rv[:, 2, :], rs[:, 0], rv[:, 3, :])
                own.link(V.scalar_tensor_tensor(rs[:, 1], rs[:, 0], -2.0, rprob[:], ALU.mult, ALU.add))
                own.link(V.tensor_reduce(rv[:, 4, :], rs[:, 1], AX.X, ALU.max))
                pick(rs[:, 1], rv[:, 4, :], rs[:, 2], rv[:, 3, :])
                own.mark(V.tensor_tensor(rv[:, 5, :], rv[:, 2, :], rv[:, 4, :], ALU.add))
                own.link(V.tensor_tensor(rs[:, 3], rs[:, 0], rs[:, 2], ALU.add))
                own.mark(V.reciprocal(rv[:, 1, :], rv[:, 5, :]))
                own.link(V.tensor_tensor(rs[:, 3], rs[:, 3], rprob[:], ALU.mult))
                V.tensor_tensor(comb[:], rs[:, 3], perx(rv[:, 1, :]), ALU.mult).then_inc(s["comb_ready"], 1)

            def copy_gates(m, first):
                dve.wait_ge(s["comb_mm"], m + 1)
                if not first:
                    dve.wait_ge(s["gates_stored"], 16 * m)
                    dve.wait_ge(s["bias_mm"], m)
                V.tensor_copy(comb_t[:], bank[7][0:E, :]).then_inc(s["comb_copied"], 1)

            def init_total(b, first):
                dve.wait_ge(s["bias_mm"], b + 1)
                if not first:
                    dve.wait_ge(s["out_turned"], b)
                V.tensor_tensor(total[:], bank[3][:], y[:], ALU.add).then_inc(s["total_init"], 1)

            def low_hidden(b, n):
                m = n % 4
                dve.wait_ge(s["relu_done"], L * b + n + 1)
                if n % 2:
                    V.tensor_copy(act_h[:, m, :], act_f[:, m, :]).then_inc(s["relu_high_v"], 1)
                    dve.wait_ge(s["relu_high_v"], L // 2 * b + n // 2 + 1)
                else:
                    dve.wait_ge(s["relu_high"], L // 2 * b + n // 2 + 1)
                V.tensor_tensor(act_l[:, m, :], act_f[:, m, :], act_h[:, m, :], ALU.subtract).then_inc(s["relu_low"], 1)

            def weigh(b, e, fresh=False):
                dve.wait_ge(s["down_mm"], L * b + FT * (e + 1))
                dve.wait_ge(gates_loaded[2 * e // E], 16 * (b + 1))
                if not (fresh and e < 2):
                    dve.wait_ge(s["added"], E * b + e - 1)
                V.tensor_tensor(weighted[:, e % 2, :], down_bank[e % 2][:], gates[:, e, :], ALU.mult)\
                    .then_inc(s["weighted_done"], 1)

            def experts(b, first, last):
                for n in range(L):
                    low_hidden(b, n)
                    if n == 1 and not first:
                        weigh(b - 1, E - 1)
                    if n >= 5 and n % FT == 1:
                        weigh(b, (n - 5) // FT, first)
                    if n == 4:
                        init_total(b, first)
                    if not last:
                        if n == 2:
                            moments_of(b + 1, "res_turned", "var1_ready")
                        if n == 4:
                            normalise(b + 1, "sd1_ready", "normed1")
                        if n == 6:
                            scale_gamma(b + 1)
                        if n == 9:
                            moments_of(b + 1, "y_turned", "var2_ready")
                        if n == 11:
                            normalise(b + 1, "sd2_ready", "normed2")
                        if n == 14:
                            centre_time(b + 1)
                        if n == 16:
                            var_time(b + 1)
                        if n == 18:
                            film_scale(b + 1)
                        if n == 23:
                            router_max(b + 1)
                        if n == 25:
                            router_pick(b + 1)
                        if n == 28:
                            copy_gates(b + 1, False)

            moments_of(0, "res_turned", "var1_ready")
            normalise(0, "sd1_ready", "normed1")
            scale_gamma(0)
            moments_of(0, "y_turned", "var2_ready")
            normalise(0, "sd2_ready", "normed2")
            centre_time(0)
            var_time(0)
            film_scale(0)
            router_max(0)
            router_pick(0)
            copy_gates(0, True)
            before = own.count
            experts(0, True, False)
            per = own.count - before
            with dve.Fori(1, NB - 1) as b:
                own.enter(b - 1, per)
                experts(b, False, False)
            own.leave(NB - 2)
            experts(NB - 1, False, True)
            weigh(NB - 1, E - 1)

        @block.scalar
        def _(act):
            A = nc.scalar
            def layer(n, dst, src, func, bias):
                act.wait_ge(s["style_mm"], n + 1)
                A.activation(dst, src, func, bias=bias).then_inc(s["style_out"], 1)

            act.wait_ge(s["params"], 19 * 16)
            act.wait_ge(s["consts3"], 2)
            act.wait_ge(s["style_mm"], 1)
            A.copy(se_t[:], bank[7][0:SE, 0:NS]).then_inc(s["style_out"], 1)
            layer(1, hyp_t[:], bank[7][:, NS:2 * NS], ACT.Relu, cols[:, HB1:HB1 + 1])
            layer(2, hyp2_t[:], bank[7][:, 2 * NS:3 * NS], ACT.Identity, cols[:, HB2:HB2 + 1])
            layer(3, sty_t[:], bank[7][0:SH2, 3 * NS:4 * NS], ACT.Relu, cols[0:SH2, SB1:SB1 + 1])
            act.wait_ge(s["style_mm"], 5)
            A.activation(film_b[:], bank[7][:, 5 * NS:6 * NS], ACT.Identity, bias=cols[:, SBT:SBT + 1])\
                .then_inc(s["act_own"], 1)
            A.activation(soft[:, 0, :], bank[7][:, 4 * NS:5 * NS], ACT.Identity, bias=cols[:, SG:SG + 1])\
                .then_inc(s["style_out"], 1)
            act.wait_ge(s["small_out"], 6)
            A.activation(soft[:, 2, :], soft[:, 2, :], ACT.Exp).then_inc(s["act_own"], 1)
            act.wait_ge(s["act_own"], 2)
            A.activation(soft[:, 1, :], soft[:, 2, :], ACT.Ln, bias=1.0).then_inc(s["style_out"], 1)

            def x_high(j):
                act.wait_ge(s["x_turned"], j + 1)
                A.copy(xh[:, j * C:(j + 1) * C], bank[6 + j % 2][:]).then_inc(s["x_high"], 1)

            def high_in(k, par, again):
                if again:
                    act.wait_ge(s["hid_mm"], k - 1)
                act.wait_ge(wi_landed[par], 8 * (k - par) + 16)
                A.copy(wh[:, par, 0:FF], wraw[:, par, 0:FF]).then_inc(s["wi_high"], 1)

            def high_out(k, par, again):
                if again:
                    act.wait_ge(s["out_mm"], k - 1)
                act.wait_ge(wo_landed[par], 8 * (k - par) + 16)
                A.copy(wh[:, par, FF:], wraw[:, par, FF:]).then_inc(s["wo_high"], 1)

            def gelu(k, par, again):
                act.wait_ge(s["hid_mm"], k + 1)
                if again:
                    act.wait_ge(s["split_done"], 2 * k - 2)
                for ft in range(FT):
                    A.activation(act_f[:, 2 * par + ft // 2, ft % 2 * CW:(ft % 2 + 1) * CW],
                                 bank[2 * par + ft // 2][:, ft % 2 * CW:(ft % 2 + 1) * CW], ACT.Gelu,
                                 bias=bi_c[:, ft, bass.ds(k, 1)]).then_inc(s["gelu_done"], 1)

            def window(k, par, more, x_next=None):
                if par == 0 and x_next is not None:
                    x_high(x_next)
                gelu(k, par, not (isinstance(k, int) and k < 2))
                if more:
                    high_in(k + 2, par, True)
                if not (isinstance(k, int) and k in (0, NW - 1)):
                    high_out(k + 1, 1 - par, True)

            x_high(0)
            high_in(0, 0, False)
            high_in(1, 1, False)
            high_out(0, 0, False)
            high_out(1, 1, False)
            for i in range(FIRST):
                window(2 * i, 0, True, i + 1 if i + 1 < NB else None)
                window(2 * i + 1, 1, True)
            with act.Fori(FIRST, NW // 2 - 1) as i:
                window(2 * i, 0, True)
                window(2 * i + 1, 1, True)
            window(NW - 3, 0, True)
            window(NW - 2, 1, False)
            window(NW - 1, 0, False)

            def high_v(e):
                par = (e + 1) % 2
                landed = 16 * ((NW + 1 - par) // 2 + e // 2 + 1)
                act.wait_ge(wi_landed[par], landed)
                act.wait_ge(wo_landed[par], landed)
                A.copy(vh[:, e, :], wraw[:, par, :]).then_inc(s["v_high"], 1)

            def fetch(m):
                act.wait_ge(s["win_done"], NW)
                A.copy(sq[:], res[:, bass.ds(m * C, C)]).then_inc(s["fetched"], 1)

            def root(m, var, done, v):
                act.wait_ge(s[var], m + 1)
                A.activation(v, v, ACT.Sqrt).then_inc(s[done], 1)

            def affine(m):
                act.wait_ge(s["back2"], m + 1)
                A.activation(t0[:], bank[7][:], ACT.Identity, bias=cols[:, LB:LB + 1], scale=cols[:, LG:LG + 1])\
                    .then_inc(s["affine"], 1)

            def square_time(m):
                act.wait_ge(s["time_centred"], m + 1)
                A.activation(sq[:], t1[:], ACT.Square).then_inc(s["time_squared"], 1)

            def high_tokens(m):
                act.wait_ge(s["film_done"], m + 1)
                A.copy(hh[:, bass.ds(m * C, C)], hf[:]).then_inc(s["h_high"], 1)

            def exp_router(m):
                act.wait_ge(s["rmax_done"], m + 1)
                A.activation(rprob[:], rprob[:], ACT.Exp).then_inc(s["exp_done"], 1)

            def copy_out(b, first):
                act.wait_ge(s["out_turned"], b + 1)
                if not first:
                    act.wait_ge(s["stored"], 16 * TB * b)
                A.copy(out_sb[:], bank[7][:].rearrange("p (t d) -> p t d", t=TB)).then_inc(s["out_copied"], 1)

            def relu(b, n, fresh):
                e, ft = divmod(n, FT)
                m = n % 4
                act.wait_ge(s["up_mm"], L * b + n + 1)
                if not (fresh and n < 4):
                    act.wait_ge(s["down_mm"], L * b + n - 3)
                A.activation(act_f[:, m, :], up_bank[n % 3][:], ACT.Relu, bias=b1_c[:, ft, e:e + 1])\
                    .then_inc(s["relu_done"], 1)
                if n % 2 == 0:
                    A.activation(act_h[:, m, :], up_bank[n % 3][:], ACT.Relu, bias=b1_c[:, ft, e:e + 1])\
                        .then_inc(s["relu_high"], 1)

            def experts(b, first, last):
                for n in range(L):
                    relu(b, n, first)
                    if first and n % FT == 1 and n // FT + 2 < E:
                        high_v(n // FT + 2)
                    if n == 4 and not first:
                        copy_out(b - 1, isinstance(b, int) and b == 1)
                    if not last:
                        if n == 0:
                            fetch(b + 1)
                        if n == 3:
                            root(b + 1, "var1_ready", "sd1_ready", spread[:])
                        if n == 10:
                            root(b + 1, "var2_ready", "sd2_ready", spread[:])
                        if n == 13:
                            affine(b + 1)
                        if n == 15:
                            square_time(b + 1)
                        if n == 17:
                            root(b + 1, "time_var", "time_sd", rt[:])
                        if n == 21:
                            high_tokens(b + 1)
                        if n == 24:
                            exp_router(b + 1)

            fetch(0)
            root(0, "var1_ready", "sd1_ready", spread[:])
            high_v(0)
            root(0, "var2_ready", "sd2_ready", spread[:])
            affine(0)
            square_time(0)
            root(0, "time_var", "time_sd", rt[:])
            high_v(1)
            high_tokens(0)
            exp_router(0)
            experts(0, True, False)
            with act.Fori(1, NB - 1) as b:
                experts(b, False, False)
            experts(NB - 1, False, True)
            copy_out(NB - 1, False)

        @block.tensor
        def _(pe):
            T = nc.tensor
            mm = T.matmul

            pe.wait_ge(s["consts2"], 1)
            pe.wait_ge(s["perm_ready"], 1)
            for q in range(SPT):
                last = mm(bank[0][:, 0:TT], part_of_quarter[:, q, :],
                          perm[:].rearrange("p (t q) -> p q t", q=SPT)[:, q, :], start=(q == 0), stop=(q == SPT - 1))
            last.then_inc(s["idx_mm"], 1)
            pe.wait_ge(s["perm_ready"], 2)
            mm(bank[1][0:E, 0:NS], hot_expert[:], perm[:], start=True, stop=True)
            mm(bank[1][0:NU, NS:2 * NS], hot_subject[:], perm[:], start=True, stop=True).then_inc(s["small_mm"], 1)
            pe.wait_ge(s["params"], 19 * 16)
            pe.wait_ge(s["small_out"], 2)
            for a in range(3):
                mm(bank[2][:, a * NS:(a + 1) * NS], gbb_r[:, a, :], sorted_expert[:], start=True, stop=True)
            for ft in range(FT):
                mm(bank[3][:, ft * NW:(ft + 1) * NW], bi_r[:, ft * P:(ft + 1) * P], win_hot_t[:], start=True, stop=True)
            for ft in range(FT):
                last = T.transpose(bank[4][:, ft * E:(ft + 1) * E], b1_r[:, ft * P:(ft + 1) * P], ident[0:E, 0:E])
            last.then_inc(s["small_mm"], 1)

            def style(n, lhs, rhs, rows):
                if n:
                    pe.wait_ge(s["style_out"], n)
                mm(bank[7][0:rows, n * NS:(n + 1) * NS], lhs, rhs, start=True, stop=True).then_inc(s["style_mm"], 1)

            style(0, emb[:], sorted_subject[:], SE)
            style(1, hw1[:], se_t[:], SH)
            style(2, hw2[:], hyp_t[:], SH)
            style(3, sw1[:], hyp2_t[:], SH2)
            pe.wait_ge(s["style_out"], 4)
            mm(bank[7][:, 4 * NS:5 * NS], sw2[:, 0:D], sty_t[:], start=True, stop=True)
            mm(bank[7][:, 5 * NS:6 * NS], sw2[:, D:2 * D], sty_t[:], start=True, stop=True).then_inc(s["style_mm"], 1)

            def turn_x(j):
                pe.wait_ge(gathered[j], 16 * TB)
                if j >= 2:
                    pe.wait_ge(s["x_ready"], 2 * (j - 1))
                for t in range(TB):
                    last = T.transpose(bank[6 + j % 2][:, t * P:(t + 1) * P], xg[:, j * TB + t, :], ident[:])
                last.then_inc(s["x_turned"], 1)

            def up(k, par, x_blocks, first=False):
                start = pe.value_load(table[0:1, 1, bass.ds(k, 1)], min_val=0, max_val=N)
                pe.wait_ge(s["x_ready"], 2 * x_blocks)
                pe.wait_ge(s["wi_high"], k + 1)
                pe.wait_ge(s["wi_low"], k + 1)
                if not first:
                    pe.wait_ge(s["gelu_done"], 4 * (k - 1))
                for ft in range(FT):
                    dst = bank[2 * par + ft // 2][:, ft % 2 * CW:(ft % 2 + 1) * CW]
                    h, l = (v[:, par, ft * P:(ft + 1) * P] for v in (wh, wl))
                    mm(dst, h, xh[:, bass.ds(start, CW)], start=True, stop=False)
                    mm(dst, h, xl[:, bass.ds(start, CW)], start=False, stop=False)
                    last = mm(dst, l, xh[:, bass.ds(start, CW)], start=False, stop=True)
                last.then_inc(s["hid_mm"], 1)

            def down(k, par, first=False):
                pe.wait_ge(s["split_done"], 2 * (k + 1))
                pe.wait_ge(s["wo_high"], k + 1)
                pe.wait_ge(s["wo_low"], k + 1)
                if not first:
                    pe.wait_ge(s["win_done"], k - 1)
                dst = down_bank[par][:, 0:CW]
                for ft in range(FT):
                    h, l = (v[:, par, FF + ft * P:FF + (ft + 1) * P] for v in (wh, wl))
                    ah, al = (v[:, 2 * par + ft // 2, ft % 2 * CW:(ft % 2 + 1) * CW] for v in (act_h, act_l))
                    mm(dst, h, ah, start=(ft == 0), stop=False)
                    mm(dst, h, al, start=False, stop=False)
                    last = mm(dst, l, ah, start=False, stop=(ft == FT - 1))
                last.then_inc(s["out_mm"], 1)

            def blocks_of(k):
                return min(NB, ((k + 1) * G + SB - 1) // SB)

            turn_x(0)
            pe.wait_ge(s["pads"], 3)
            up(0, 0, 1, True)
            for i in range(FIRST):
                if i + 1 < NB:
                    turn_x(i + 1)
                up(2 * i + 1, 1, blocks_of(2 * i + 1), i == 0)
                down(2 * i, 0, i == 0)
                up(2 * i + 2, 0, blocks_of(2 * i + 2))
                down(2 * i + 1, 1, i == 0)
            with pe.Fori(FIRST, NW // 2) as i:
                up(2 * i + 1, 1, NB)
                down(2 * i, 0)
                up(2 * i + 2, 0, NB)
                down(2 * i + 1, 1)
            down(NW - 1, 0)

            def turn(m, src, ready, dst, done):
                pe.wait_ge(s[ready], m + 1)
                for t in range(TB):
                    last = T.transpose(dst[:, t * P:(t + 1) * P], src(t), ident[:])
                last.then_inc(s[done], 1)

            def turn_res(m):
                pe.wait_ge(s["fetched"], m + 1)
                for t in range(TB):
                    last = T.transpose(bank[6][:, t * P:(t + 1) * P], sq[:, t * P:(t + 1) * P], ident[:])
                last.then_inc(s["res_turned"], 1)

            def route(m):
                pe.wait_ge(s["film_done"], m + 1)
                for t in range(TB):
                    last = mm(bank[6][:, t * E:(t + 1) * E], hf[:, t * P:(t + 1) * P], rw[:], start=True, stop=True)
                last.then_inc(s["logits_mm"], 1)

            def turn_gates(m):
                pe.wait_ge(s["comb_ready"], m + 1)
                for t in range(TB):
                    last = T.transpose(bank[7][0:E, t * P:(t + 1) * P], comb[:, t, :], ident[:])
                last.then_inc(s["comb_mm"], 1)

            def bias_out(m, first):
                pe.wait_ge(s["comb_copied"], m + 1)
                if not first:
                    pe.wait_ge(s["total_init"], m)
                mm(bank[3][:], b2_r[:], comb_t[:], start=True, stop=True).then_inc(s["bias_mm"], 1)

            def up_v(b, n, fresh=False):
                e, ft = divmod(n, FT)
                if n == 0:
                    pe.wait_ge(s["h_low"], b + 1)
                if fresh:
                    pe.wait_ge(s["v_low"], e + 1)
                before = n - 3 if n >= 3 else (30, 31, 29)[n] - L
                if not (fresh and n < 3):
                    pe.wait_ge(s["relu_done"], L * b + before + 1)
                    if before % 2 == 0:
                        pe.wait_ge(s["relu_high"], L // 2 * b + before // 2 + 1)
                h, l = (v[:, e, ft * P:(ft + 1) * P] for v in (vh, vl))
                th, tl = (v[:, bass.ds(b * C, C)] for v in (hh, hl))
                mm(up_bank[n % 3][:], h, th, start=True, stop=False)
                mm(up_bank[n % 3][:], h, tl, start=False, stop=False)
                mm(up_bank[n % 3][:], l, th, start=False, stop=True).then_inc(s["up_mm"], 1)

            def down_v(b, n, fresh):
                e, ft = divmod(n, FT)
                if ft == 0 and not (fresh and e < 2):
                    pe.wait_ge(s["weighted_done"], E * b + e - 1)
                pe.wait_ge(s["relu_low"], L * b + n + 1)
                h, l = (v[:, e, FF + ft * P:FF + (ft + 1) * P] for v in (vh, vl))
                dst, m = down_bank[e % 2][:], n % 4
                mm(dst, h, act_h[:, m, :], start=(ft == 0), stop=False)
                mm(dst, h, act_l[:, m, :], start=False, stop=False)
                mm(dst, l, act_h[:, m, :], start=False, stop=(ft == FT - 1)).then_inc(s["down_mm"], 1)

            def turn_total(b):
                pe.wait_ge(s["added"], E * (b + 1))
                for t in range(TB):
                    last = T.transpose(bank[7][:, t * P:(t + 1) * P], total[:, t * P:(t + 1) * P], ident[:])
                last.then_inc(s["out_turned"], 1)

            tile_of = lambda v: lambda t: v[:, t * P:(t + 1) * P]
            normal_of = lambda t: normal[:, t, :]

            def experts(b, first, last):
                for n in range(L):
                    if n + 2 < L:
                        up_v(b, n + 2, first)
                    elif not last:
                        up_v(b + 1, n + 2 - L)
                    down_v(b, n, first)
                    if n == 3 and not first:
                        turn_total(b - 1)
                    if not last:
                        if n == 1:
                            turn_res(b + 1)
                        if n == 5:
                            if not first:
                                pe.wait_ge(s["out_copied"], b)
                            turn(b + 1, normal_of, "normed1", bank[7], "back1")
                        if n == 8:
                            turn(b + 1, tile_of(y), "y_ready", bank[6], "y_turned")
                        if n == 12:
                            turn(b + 1, normal_of, "normed2", bank[7], "back2")
                        if n == 22:
                            route(b + 1)
                        if n == 27:
                            turn_gates(b + 1)
                        if n == 30:
                            bias_out(b + 1, False)

            pe.wait_ge(s["win_done"], NW)
            turn_res(0)
            turn(0, normal_of, "normed1", bank[7], "back1")
            turn(0, tile_of(y), "y_ready", bank[6], "y_turned")
            turn(0, normal_of, "normed2", bank[7], "back2")
            route(0)
            turn_gates(0)
            bias_out(0, True)
            up_v(0, 0, True)
            up_v(0, 1, True)
            experts(0, True, False)
            with pe.Fori(1, NB - 1) as b:
                experts(b, False, False)
            experts(NB - 1, False, True)
            turn_total(NB - 1)


_INS = ['x', 'itok_B_0_7', 'itok_B_6_14', 'L0_cond_Wi', 'L0_cond_bi', 'L0_cond_Wo', 'L0_cond_bo', 'L0_cond_gamma',
        'L0_cond_beta', 'L1_cond_ln_g', 'L1_cond_ln_b', 'L1_cond_subj_emb', 'L1_cond_hyp_w1', 'L1_cond_hyp_b1',
        'L1_cond_hyp_w2', 'L1_cond_hyp_b2', 'L1_cond_sty_w1', 'L1_cond_sty_b1', 'L1_cond_sty_w2', 'L1_cond_sty_b2',
        'L1_cond_router_w', 'L1_cond_exp_w1', 'L1_cond_exp_b1', 'L1_cond_exp_w2', 'L1_cond_exp_b2']


def kernel(**inputs):
    import numpy as _np
    import concourse.bacc as _bacc
    from concourse import mybir as _mybir
    from concourse.bass_utils import run_bass_kernel_spmd as _run

    nc = _bacc.Bacc("TRN2", target_bir_lowering=False, num_devices=1)
    arrays, args = {}, []
    for name in _INS:
        a = _np.ascontiguousarray(inputs[name])
        arrays[f"in_{name}_dram"] = a
        args.append(nc.dram_tensor(f"in_{name}_dram", a.shape, _mybir.dt.from_np(a.dtype), kind="ExternalInput").ap())
    args.append(nc.dram_tensor("out_0_dram", inputs["x"].shape, _mybir.dt.float32, kind="ExternalOutput").ap())
    build(nc, *args)
    r = _run(nc, [arrays], core_ids=[0])
    return r.results[0]["out_0_dram"]
```

```python
from contextlib import ExitStack

import concourse.bass as bass
from concourse import mybir

F32 = mybir.dt.float32
F32R = mybir.dt.float32r
I32 = mybir.dt.int32
ALU = mybir.AluOpType
ACT = mybir.ActivationFunctionType
AX = mybir.AxisListType

P = 128


class Chain:

    def __init__(self, engine, semaphore):
        self.engine, self.semaphore, self.count, self.extra = engine, semaphore, 0, 0

    def mark(self, instruction):
        self.count += 1
        instruction.then_inc(self.semaphore, 1)

    def link(self, instruction):
        self.mark(instruction)
        self.engine.wait_ge(self.semaphore, self.count + self.extra)

    def enter(self, i, per_turn):
        self.start, self.per_turn, self.extra = self.count, per_turn, i * per_turn

    def leave(self, turns):
        assert self.count - self.start == self.per_turn, (self.count - self.start, self.per_turn)
        self.count, self.extra = self.start + turns * self.per_turn, 0


def build(nc, x, expert_of, subject_of, Wi, bi, Wo, bo, gamma, beta, ln_g, ln_b, subj_emb, hyp_w1, hyp_b1,
          hyp_w2, hyp_b2, sty_w1, sty_b1, sty_w2, sty_b2, router_w, exp_w1, exp_b1, exp_w2, exp_b2, out):
    NS, S, D = x.shape
    E, _, FF = Wi.shape
    NU, SE = subj_emb.shape
    SH, SH2 = sty_w1.shape
    N = NS * S
    FT = FF // P
    TT = N // P
    SPT = P // S
    C = 512
    NB = N // C
    SB = C // S
    TB = C // P
    G = 8
    CW = G * S
    NW = (NS - E) // G + E
    assert D == P and NW % 2 == 1
    NP = N + CW

    x_rows = x.rearrange("s t d -> (s t) d")
    out_rows = out.rearrange("s t d -> (s t) d")
    gate_rows = nc.dram_tensor("gate_rows", [NB, E * C], F32, kind="Internal").ap()

    def col(v):
        return v.rearrange("(p o) -> p o", o=1)

    with ExitStack() as ctx:
        def sb(name, shape, dt=F32):
            return ctx.enter_context(nc.sbuf_tensor(name, shape, dt))

        def sem(name):
            return ctx.enter_context(nc.semaphore(name))

        bank = [ctx.enter_context(nc.psum_tensor(f"bank{i}", [P, 512], F32)) for i in range(8)]

        ident = sb("ident", [P, P])
        iota_row = sb("iota_row", [P, NS])
        iota_part = sb("iota_part", [P, 1])
        iota_diag = sb("iota_diag", [P, P])
        total = sb("total", [P, C])
        part_of_quarter = total[0:NS, :].rearrange("p (q n) -> p q n", q=SPT)
        minus_half = sb("minus_half", [P, SB])
        fetched_y = sb("fetched_y", [P, C])
        zero_cols = fetched_y[:, 0:CW]

        ids_all = sb("ids_all", [P, NS], I32)
        ids_col = sb("ids_col", [NS, 2], I32)
        key_all = sb("key_all", [P, NS])
        key_col = sb("key_col", [NS, 1])
        idf_all = sb("idf_all", [P, NS])
        idf_col = sb("idf_col", [NS, 2])
        smaller = sb("smaller", [NS, NS])
        place = sb("place", [NS, 1])
        perm = sb("perm", [NS, NS])
        below = sb("below", [P, E + 1, NS])
        out_sb = below[:].rearrange("p e n -> p (e n)")[:, 0:C].rearrange("p (t d) -> p t d", d=D)
        first_of = sb("first_of", [P, E + 1])
        number = sb("number", [P, E])
        steps_cmp = sb("steps_cmp", [P, E, G])
        windows = sb("windows", [P, E])
        upto_mask = sb("upto_mask", [P, E, E])
        upto_part = sb("upto_part", [P, E, E])
        windows_in = sb("windows_in", [P, E])
        base_val = sb("base_val", [P, E])
        win_cmp = sb("win_cmp", [P, NW, E])
        win_expert = sb("win_expert", [P, NW])
        win_hot = sb("win_hot", [P, NW, E])
        win_part = sb("win_part", [P, NW, E])
        win_start = sb("win_start", [P, NW])
        table = sb("table", [1, 2, NW], I32)
        hot_expert = sb("hot_expert", [NS, E])
        hot_subject = sb("hot_subject", [NS, NU])
        win_hot_t = sb("win_hot_t", [E, NW])
        row_index = sb("row_index", [P, TT], I32)
        part_in_sample = sb("part_in_sample", [P, 1])
        sorted_expert = sb("sorted_expert", [E, NS])
        sorted_subject = sb("sorted_subject", [NU, NS])

        bi_r = sb("bi_r", [E, FF])
        b1_r = sb("b1_r", [E, FF])
        b2_r = sb("b2_r", [E, D])
        gbb_r = sb("gbb_r", [E, 3, D])
        cols = sb("cols", [P, 7])
        HB1, HB2, SB1, SG, SBT, LG, LB = range(7)
        emb = sb("emb", [NU, SE])
        hw1 = sb("hw1", [SE, SH])
        hw2 = sb("hw2", [SH, SH])
        sw1 = sb("sw1", [SH, SH2])
        sw2 = sb("sw2", [SH2, 2 * D])
        rw = sb("rw", [D, E])
        per_sample = sb("per_sample", [P, 3, NS])
        bi_c = sb("bi_c", [P, FT, NW])
        b1_c = sb("b1_c", [P, FT, E])
        se_t = sb("se_t", [SE, NS])
        hyp_t = sb("hyp_t", [SH, NS])
        hyp2_t = sb("hyp2_t", [SH, NS])
        sty_t = sb("sty_t", [SH2, NS])
        film_a = sb("film_a", [P, NS])
        film_b = sb("film_b", [P, NS])
        soft = sb("soft", [P, 3, NS])

        early = sb("early", [P, TT * D + NP])
        xg = early[:, 0:TT * D].rearrange("p (t d) -> p t d", d=D)
        xh = sb("xh", [P, NP], F32R)
        xl = sb("xl", [P, NP], F32R)
        xb = early[:, TT * D:]
        res = sb("res", [P, NP])
        wraw = sb("wraw", [P, 2, 2 * FF])
        wih = sb("wih", [P, 2, FF], F32R)
        wil = sb("wil", [P, 2, FF], F32R)
        woh = sb("woh", [P, 3, FF], F32R)
        wol = sb("wol", [P, 3, FF], F32R)
        act_f = sb("act_f", [P, 4, C])
        act_h = sb("act_h", [P, 4, C], F32R)
        act_l = sb("act_l", [P, 4, C], F32R)

        vh = sb("vh", [P, E, 2 * FF], F32R)
        vl = sb("vl", [P, E, 2 * FF], F32R)
        fetched_res = sb("fetched_res", [P, C])
        scaled = sb("scaled", [P, C])
        t0 = sb("t0", [P, C])
        t1 = sb("t1", [P, C])
        sq = sb("sq", [P, C])
        hf = sb("hf", [P, C])
        hh, hl = xh, xl
        stats = [sb(f"stats{i}", [P, TB, 6]) for i in (1, 2)]
        moments = [sb(f"moments{i}", [P, TB, 2]) for i in (1, 2)]
        spread = [sb(f"spread{i}", [P, TB]) for i in (1, 2)]
        normal = [sb(f"normal{i}", [P, TB, D]) for i in (1, 2)]
        scratch = sb("scratch", [P, 1])
        carrier = sb("carrier", [P, 1])
        block_index = sb("block_index", [P, TB], I32)
        sums = sb("sums", [P, SB])
        rt = sb("rt", [P, SB])
        rmax = sb("rmax", [P, TB])
        rprob = sb("rprob", [P, TB, E])
        rs = sb("rs", [P, 4, TB, E])
        rv = sb("rv", [P, 6, TB])
        comb = sb("comb", [P, TB, E])
        comb_t = sb("comb_t", [E, C])
        gates = early[:, 0:E * C].rearrange("p (e c) -> p e c", e=E)
        weighted = sb("weighted", [P, 2, C])

        names = """ids params params_late consts consts2 idx_mm idx_ready perm_ready hot_ready table_ready dve_own dve_first act_own pool_own
            small_mm small_out style_mm style_out x_turned x_high x_ready pads
            wi_high wo_high wi_low wi_low_pool wo_low wo_low_pool hid_mm gelu_done split_high split_low out_mm win_done
            v_high v_low res_turned var1_ready rstd1_ready normed1 back1 scaled1 y_ready y_turned var2_ready
            rstd2_ready normed2 back2 affine time_centred time_squared time_var res_fetched fetched film_a_ready time_root x_read film_done h_high h_low
            logits_mm rmax_done exp_done comb_ready comb_mm comb_copied gates_stored bias_mm total_init
            up_mm relu_done relu_high relu_high_v relu_low down_mm weighted_done added out_turned out_copied
            index_copied stored"""
        s = {name: sem(name) for name in names.split()}
        gathered = [sem(f"gathered{j}") for j in range(NB)]
        wi_landed = [sem("wi_landed0"), sem("wi_landed1")]
        wo_landed = [sem("wo_landed0"), sem("wo_landed1")]
        gates_loaded = [sem("gates_loaded0"), sem("gates_loaded1")]
        v_landed = [sem("v_landed0"), sem("v_landed1")]
        block = ctx.enter_context(nc.Block())

        L = E * FT
        whole = lambda m: ((m + 1) * SB - E) // G + E
        norm1_bank = (6, 7, 3, 3)
        STEPS = 2 * NW
        LAG = 3
        in_on_pool = lambda k: k >= 6
        out_on_pool = lambda k: k >= 2
        high_on_act = lambda n: n % 8 in (0, 1, 2, 4, 6)
        highs_by_act = lambda n: sum(high_on_act(i) for i in range(n + 1))
        highs_by_dve = lambda n: n + 1 - highs_by_act(n)
        ACT_HIGHS, DVE_HIGHS = highs_by_act(L - 1), highs_by_dve(L - 1)
        up_bank = [bank[0], bank[1], bank[2]]
        down_bank = [bank[4], bank[5]]

        def low_of(k, which):
            names, pool_has = {"in": (("wi_low", "wi_low_pool"), in_on_pool), "out": (("wo_low", "wo_low_pool"), out_on_pool)}[which]
            return s[names[pool_has(k)]], sum(pool_has(j) == pool_has(k) for j in range(k + 1))

        @block.sync
        def _(sp):
            sp.dma_start(ids_all[:], expert_of.partition_broadcast(P)).then_inc(s["ids"], 16)
            sp.dma_start(ids_col[:, 0:1], col(expert_of)).then_inc(s["ids"], 16)
            sp.dma_start(ids_col[:, 1:2], col(subject_of)).then_inc(s["ids"], 16)
            for dst, src in ((b1_r[:], exp_b1), (b2_r[:], exp_b2), (rw[:], router_w),
                             (cols[:, LG:LG + 1], col(ln_g)), (cols[:, LB:LB + 1], col(ln_b))):
                sp.dma_start(dst, src).then_inc(s["params_late"], 16)
            sp.wait_ge(s["table_ready"], 1)

            for k in range(NW):
                par = k % 2
                e = sp.value_load(table[0:1, 0, k:k + 1], min_val=0, max_val=E - 1)
                if k >= 2:
                    sp.wait_ge(s["wi_high"], k - 1)
                    sp.wait_ge(*low_of(k - 2, "in"))
                sp.dma_start(wraw[:, par, 0:FF], Wi[bass.ds(e, 1), :, :].rearrange("o p f -> p (o f)"))\
                    .then_inc(wi_landed[par], 16)
                if k >= 2:
                    sp.wait_ge(s["wo_high"], k - 1)
                    sp.wait_ge(*low_of(k - 2, "out"))
                sp.dma_start(wraw[:, par, FF:2 * FF].rearrange("p (t d) -> p t d", t=FT),
                             Wo[bass.ds(e, 1), :, :].rearrange("o (t p) d -> p (o t) d", p=P))\
                    .then_inc(wo_landed[par], 16)

            def load_v(e):
                par = (e + 1) % 2
                if e < 2:
                    sp.wait_ge(s["wi_high"], NW - 1 + e)
                    sp.wait_ge(s["wo_high"], NW - 1 + e)
                    sp.wait_ge(*low_of(NW - 2 + e, "in"))
                    sp.wait_ge(*low_of(NW - 2 + e, "out"))
                else:
                    sp.wait_ge(s["v_high"], e - 1)
                    sp.wait_ge(s["v_low"], e - 1)
                sp.dma_start(wraw[:, par, 0:FF], exp_w1[e]).then_inc(wi_landed[par], 16)
                sp.dma_start(wraw[:, par, FF:2 * FF].rearrange("p (t d) -> p t d", t=FT),
                             exp_w2[e].rearrange("(t p) d -> p t d", p=P)).then_inc(wo_landed[par], 16)

            def gates_trip(b):
                sp.wait_ge(s["comb_copied"], b + 1)
                sp.dma_start(gate_rows[b:b + 1, :].rearrange("o (e c) -> (o e) c", e=E), comb_t[:])\
                    .then_inc(s["gates_stored"], 16)
                sp.wait_ge(s["gates_stored"], 16 * (b + 1))
                for half in range(2):
                    if b:
                        sp.wait_ge(s["weighted_done"], E * (b - 1) + E // 2 * (half + 1))
                    w = E * C // 2
                    sp.dma_start(gates[:, half * E // 2:(half + 1) * E // 2, :].rearrange("p e c -> p (e c)"),
                                 gate_rows[b, half * w:(half + 1) * w].partition_broadcast(P))\
                        .then_inc(gates_loaded[half], 16)

            load_v(0)
            load_v(1)
            load_v(2)
            load_v(3)
            gates_trip(0)
            for e in range(4, E):
                load_v(e)
            for b in range(1, NB):
                gates_trip(b)

        @block.gpsimd
        def _(pool):
            own = Chain(pool, s["pool_own"])
            nc.gpsimd.iota(iota_row[:], pattern=[[1, NS]], base=0, channel_multiplier=0,
                           allow_small_or_imprecise_dtypes=True).then_inc(s["consts"], 1)
            nc.gpsimd.iota(iota_part[:], pattern=[[1, 1]], base=0, channel_multiplier=1,
                           allow_small_or_imprecise_dtypes=True).then_inc(s["consts"], 1)
            nc.gpsimd.iota(iota_diag[:], pattern=[[1, P]], base=0, channel_multiplier=-1,
                           allow_small_or_imprecise_dtypes=True).then_inc(s["consts"], 1)
            nc.gpsimd.iota(upto_mask[:], pattern=[[1, E], [-1, E]], base=0, channel_multiplier=0,
                           allow_small_or_imprecise_dtypes=True).then_inc(s["consts"], 1)
            own.link(nc.gpsimd.memset(part_of_quarter, 0.0))
            for q in range(SPT):
                own.link(nc.gpsimd.iota(part_of_quarter[:, q, q * S:(q + 1) * S], pattern=[[0, S]], base=0,
                                        channel_multiplier=S, allow_small_or_imprecise_dtypes=True))
                own.link(nc.gpsimd.iota(part_in_sample[q * S:(q + 1) * S, :], pattern=[[1, 1]], base=0,
                                        channel_multiplier=1, allow_small_or_imprecise_dtypes=True))
            nc.gpsimd.memset(scratch[:], 0.0).then_inc(s["consts2"], 1)
            nc.gpsimd.memset(minus_half[:], -0.5)
            own.link(nc.gpsimd.memset(zero_cols, 0.0))
            nc.gpsimd.tensor_copy(xh[:, N:NP], zero_cols).then_inc(s["pads"], 1)
            nc.gpsimd.tensor_copy(xl[:, N:NP], zero_cols).then_inc(s["pads"], 1)
            nc.gpsimd.tensor_copy(xb[:, N:NP], zero_cols).then_inc(s["pads"], 1)

            def gather(j):
                for t in range(j * TB, (j + 1) * TB):
                    pool.indirect_dma_start(xg[:, t, :], None, x_rows,
                                            bass.IndirectOffsetOnAxis(row_index[:, t:t + 1], 0)).then_inc(gathered[j], 16)

            def low_in(k):
                pool.wait_ge(s["hid_mm"], 2 * k - 2)
                pool.wait_ge(wi_landed[k % 2], 16 * (k // 2 + 1))
                pool.wait_ge(s["wi_high"], k + 1)
                nc.gpsimd.tensor_tensor(wil[:, k % 2, :], wraw[:, k % 2, 0:FF], wih[:, k % 2, :], ALU.subtract)\
                    .then_inc(s["wi_low_pool"], 1)

            def low_out(k):
                if k >= 3:
                    pool.wait_ge(s["out_mm"], 2 * k - 4)
                pool.wait_ge(wo_landed[k % 2], 16 * (k // 2 + 1))
                pool.wait_ge(s["wo_high"], k + 1)
                nc.gpsimd.tensor_tensor(wol[:, k % 3, :], wraw[:, k % 2, FF:], woh[:, k % 3, :], ALU.subtract)\
                    .then_inc(s["wo_low_pool"], 1)

            def root(m, norm):
                pool.wait_ge(s[f"var{norm}_ready"], m + 1)
                v = spread[norm - 1][:]
                nc.gpsimd.tensor_tensor(v, v, minus_half[:, 0:TB], ALU.pow).then_inc(s[f"rstd{norm}_ready"], 1)

            def root_time(m):
                pool.wait_ge(s["time_var"], m + 1)
                nc.gpsimd.tensor_tensor(rt[:], rt[:], minus_half[:], ALU.pow).then_inc(s["time_root"], 1)

            samples = lambda v: v.rearrange("p (a n) -> p a n", n=S)
            each = lambda v: v.unsqueeze(2).to_broadcast([P, SB, S])

            def add_beta(m):
                pool.wait_ge(s["scaled1"], m + 1)
                nc.gpsimd.tensor_tensor(samples(res[:, m * C:(m + 1) * C]), samples(scaled[:]),
                                        each(per_sample[:, 1, m * SB:(m + 1) * SB]), ALU.add).then_inc(s["y_ready"], 1)

            pool.wait_ge(s["idx_ready"], 1)
            for j in range(NB):
                gather(j)
            for k in range(NW):
                if in_on_pool(k):
                    low_in(k)
                if k >= 1 and out_on_pool(k - 1):
                    low_out(k - 1)
                if k == NW - 2:
                    root(0, 1)
            low_out(NW - 1)

            def low_v(e):
                pool.wait_ge(s["v_high"], e + 1)
                nc.gpsimd.tensor_tensor(vl[:, e, :], wraw[:, (e + 1) % 2, :], vh[:, e, :], ALU.subtract)\
                    .then_inc(s["v_low"], 1)

            def low_tokens(m):
                pool.wait_ge(s["h_high"], m + 1)
                nc.gpsimd.tensor_tensor(hl[:, bass.ds(m * C, C)], hf[:], hh[:, bass.ds(m * C, C)], ALU.subtract)\
                    .then_inc(s["h_low"], 1)

            def add(b, e):
                pool.wait_ge(s["weighted_done"], E * b + e + 1)
                if e:
                    pool.wait_ge(s["added"], E * b + e)
                else:
                    pool.wait_ge(s["total_init"], b + 1)
                nc.gpsimd.tensor_tensor(total[:], total[:], weighted[:, e % 2, :], ALU.add).then_inc(s["added"], 1)

            def scatter(b):
                pool.wait_ge(s["out_copied"], b + 1)
                nc.gpsimd.tensor_copy(block_index[:], row_index[:, bass.ds(b * TB, TB)]).then_inc(s["index_copied"], 1)
                pool.wait_ge(s["index_copied"], b + 1)
                nc.gpsimd.tensor_tensor(scratch[:], scratch[:], scratch[:], ALU.add)
                for t in range(TB):
                    pool.indirect_dma_start(out_rows, bass.IndirectOffsetOnAxis(block_index[:, t:t + 1], 0),
                                            out_sb[:, t, :], None).then_inc(s["stored"], 16)

            def experts(b, first, last):
                if first:
                    low_v(2)
                    low_v(3)
                else:
                    add(b - 1, E - 2)
                    add(b - 1, E - 1)
                if not last:
                    root(b + 1, 2)
                if not first:
                    scatter(b - 1)
                for e in range(E - 2):
                    add(b, e)
                    if first and e == 1:
                        root(3, 1)
                    if first and e == 3:
                        add_beta(3)
                    if first and e + 4 < E:
                        low_v(e + 4)
                    if e == 2 and not last:
                        root_time(b + 1)
                    if e == 3 and not last:
                        low_tokens(b + 1)

            add_beta(0)
            root(1, 1)
            root(0, 2)
            low_v(0)
            add_beta(1)
            root(2, 1)
            root_time(0)
            low_tokens(0)
            add_beta(2)
            low_v(1)
            experts(0, True, False)
            with pool.Fori(1, NB - 1) as b:
                experts(b, False, False)
            experts(NB - 1, False, True)
            add(NB - 1, E - 2)
            add(NB - 1, E - 1)
            scatter(NB - 1)
            pool.wait_ge(s["stored"], 16 * TT)

        @block.vector
        def _(dve):
            own = Chain(dve, s["dve_own"])
            V = nc.vector

            dve.wait_ge(s["consts"], 4)
            dve.wait_ge(s["ids"], 48)
            own.mark(V.tensor_copy(idf_all[:], ids_all[:]))
            own.mark(V.tensor_scalar(ident[:], iota_diag[:], 0.0, None, ALU.is_equal))
            own.link(V.tensor_copy(idf_col[:], ids_col[:]))
            own.mark(V.scalar_tensor_tensor(key_all[:], idf_all[:], float(NS), iota_row[:], ALU.mult, ALU.add))
            own.link(V.scalar_tensor_tensor(key_col[:], idf_col[:, 0:1], float(NS), iota_part[0:NS, :], ALU.mult, ALU.add))
            own.link(V.tensor_scalar(smaller[:], key_all[0:NS, :], key_col[:, 0:1], None, ALU.is_lt))
            own.link(V.tensor_reduce(place[:], smaller[:], AX.X, ALU.add))
            V.tensor_scalar(perm[:], iota_row[0:NS, :], place[:, 0:1], None, ALU.is_equal).then_inc(s["perm_ready"], 1)
            V.tensor_scalar(hot_expert[:], iota_row[0:NS, 0:E], idf_col[:, 0:1], None, ALU.is_equal)\
                .then_inc(s["perm_ready"], 1)
            V.tensor_scalar(hot_subject[:], iota_row[0:NS, 0:NU], idf_col[:, 1:2], None, ALU.is_equal)\
                .then_inc(s["perm_ready"], 1)

            dve.wait_ge(s["idx_mm"], 1)
            V.tensor_scalar(row_index[:], bank[0][:, 0:TT], part_in_sample[:, 0:1], None, ALU.add)\
                .then_inc(s["idx_ready"], 1)

            own.link(V.tensor_tensor(below[:], idf_all[:].unsqueeze(1).to_broadcast([P, E + 1, NS]),
                                     iota_row[:, 0:E + 1].unsqueeze(2).to_broadcast([P, E + 1, NS]), ALU.is_lt))
            own.link(V.tensor_reduce(first_of[:], below[:], AX.X, ALU.add))
            own.link(V.tensor_tensor(number[:], first_of[:, 1:E + 1], first_of[:, 0:E], ALU.subtract))
            steps = iota_row[:, 0:NS].rearrange("p (a g) -> p g a", g=G)[:, 0, 0:G]
            own.link(V.tensor_tensor(steps_cmp[:], number[:].unsqueeze(2).to_broadcast([P, E, G]),
                                     steps.unsqueeze(1).to_broadcast([P, E, G]), ALU.is_gt))
            own.link(V.tensor_reduce(windows[:], steps_cmp[:], AX.X, ALU.add))
            own.link(V.tensor_scalar(upto_part[:], upto_mask[:], 0.0, None, ALU.is_ge))
            own.link(V.tensor_tensor(upto_part[:], upto_part[:], windows[:].unsqueeze(1).to_broadcast([P, E, E]), ALU.mult))
            own.link(V.tensor_reduce(windows_in[:], upto_part[:], AX.X, ALU.add))
            own.link(V.tensor_tensor(base_val[:], windows_in[:], windows[:], ALU.subtract))
            own.link(V.scalar_tensor_tensor(base_val[:], base_val[:], -float(G), first_of[:, 0:E], ALU.mult, ALU.add))
            own.link(V.tensor_tensor(win_cmp[:], windows_in[:].unsqueeze(1).to_broadcast([P, NW, E]),
                                     iota_row[:, 0:NW].unsqueeze(2).to_broadcast([P, NW, E]), ALU.is_le))
            own.link(V.tensor_reduce(win_expert[:], win_cmp[:], AX.X, ALU.add))
            own.link(V.tensor_scalar(win_expert[:], win_expert[:], float(E - 1), None, ALU.min))
            V.tensor_scalar(win_hot_t[:], win_expert[0:E, :], iota_part[0:E, 0:1], None, ALU.is_equal)\
                .then_inc(s["hot_ready"], 1)
            own.link(V.tensor_tensor(win_hot[:], iota_row[:, 0:E].unsqueeze(1).to_broadcast([P, NW, E]),
                                     win_expert[:].unsqueeze(2).to_broadcast([P, NW, E]), ALU.is_equal))
            own.link(V.tensor_tensor(win_part[:], win_hot[:], base_val[:].unsqueeze(1).to_broadcast([P, NW, E]), ALU.mult))
            own.link(V.tensor_reduce(win_start[:], win_part[:], AX.X, ALU.add))
            own.link(V.scalar_tensor_tensor(win_start[:], iota_row[:, 0:NW], float(G), win_start[:], ALU.mult, ALU.add))
            own.link(V.tensor_scalar(win_start[:], win_start[:], float(NS), float(S), ALU.min, ALU.mult))
            own.link(V.tensor_copy(table[:, 0, :], win_expert[0:1, :]))
            V.tensor_copy(table[:, 1, :], win_start[0:1, :]).then_inc(s["table_ready"], 1)

            def x_block(j):
                dve.wait_ge(s["x_high"], j + 1)
                bk = bank[6 + j % 2]
                V.tensor_tensor(xl[:, j * C:(j + 1) * C], bk[:], xh[:, j * C:(j + 1) * C], ALU.subtract)\
                    .then_inc(s["x_ready"], 1)
                if j == 0:
                    dve.wait_ge(s["small_out"], 3)
                V.tensor_tensor(xb[:, j * C:(j + 1) * C].rearrange("p (a n) -> p a n", n=S),
                                bk[:].rearrange("p (a n) -> p a n", n=S),
                                per_sample[:, 2, j * SB:(j + 1) * SB].unsqueeze(2).to_broadcast([P, SB, S]),
                                ALU.add).then_inc(s["x_read"], 1)

            def low_in(k):
                if k >= 2:
                    dve.wait_ge(s["hid_mm"], 2 * k - 2)
                dve.wait_ge(wi_landed[k % 2], 16 * (k // 2 + 1))
                dve.wait_ge(s["wi_high"], k + 1)
                V.tensor_tensor(wil[:, k % 2, :], wraw[:, k % 2, 0:FF], wih[:, k % 2, :], ALU.subtract)\
                    .then_inc(s["wi_low"], 1)

            def low_out(k):
                dve.wait_ge(wo_landed[k % 2], 16 * (k // 2 + 1))
                dve.wait_ge(s["wo_high"], k + 1)
                V.tensor_tensor(wol[:, k % 3, :], wraw[:, k % 2, FF:], woh[:, k % 3, :], ALU.subtract)\
                    .then_inc(s["wo_low"], 1)

            def split(j):
                dve.wait_ge(s["gelu_done"], 2 * (j + 1))
                a, h, l = (v[:, j % 4, :] for v in (act_f, act_h, act_l))
                V.tensor_copy(h, a).then_inc(s["split_high"], 1)
                dve.wait_ge(s["split_high"], j + 1)
                V.tensor_tensor(l, a, h, ALU.subtract).then_inc(s["split_low"], 1)

            def finish(k):
                start = dve.value_load(table[0:1, 1, k:k + 1], min_val=0, max_val=N)
                if k:
                    dve.wait_ge(s["win_done"], k)
                dve.wait_ge(s["out_mm"], 2 * (k + 1))
                V.tensor_tensor(res[:, bass.ds(start, CW)], down_bank[k % 2][:, 0:CW], xb[:, bass.ds(start, CW)], ALU.add)\
                    .then_inc(s["win_done"], 1)

            samples = lambda v: v.rearrange("p (a n) -> p a n", n=S)
            each = lambda v: v.unsqueeze(2).to_broadcast([P, SB, S])
            tiles = lambda v: v.rearrange("p (t d) -> p t d", t=TB)
            perx = lambda v: v.unsqueeze(2).to_broadcast([P, TB, E])

            def norm_bank(m, norm):
                return bank[6 if norm == 2 else norm1_bank[m]]

            def moments_of(m, norm, own=own):
                dve.wait_ge(s["res_turned" if norm == 1 else "y_turned"], m + 1)
                for t in range(TB):
                    own.mark(V.bn_stats(stats[norm - 1][:, t, :], tiles(norm_bank(m, norm)[:])[:, t, :]))
                dve.wait_ge(own.semaphore, own.count + own.extra)
                V.tensor_copy(carrier[:], iota_part[:])
                for t in range(TB):
                    own.mark(V.bn_aggr(moments[norm - 1][:, t, :], stats[norm - 1][:, t, :]))
                dve.wait_ge(own.semaphore, own.count + own.extra)
                V.tensor_scalar(spread[norm - 1][:], moments[norm - 1][:, :, 1], {1: 1e-12, 2: 1e-5}[norm], None, ALU.add)\
                    .then_inc(s[f"var{norm}_ready"], 1)

            def normalise(m, norm):
                dve.wait_ge(s[f"rstd{norm}_ready"], m + 1)
                if not (isinstance(m, int) and m == 0):
                    dve.wait_ge(s[f"back{norm}"], m)
                for t in range(TB):
                    ins = V.tensor_scalar(normal[norm - 1][:, t, :], tiles(norm_bank(m, norm)[:])[:, t, :],
                                          moments[norm - 1][:, t, 0:1], spread[norm - 1][:, t:t + 1],
                                          ALU.subtract, ALU.mult)
                ins.then_inc(s[f"normed{norm}"], 1)

            def scale_gamma(m):
                dve.wait_ge(s["back1"], m + 1)
                if m:
                    dve.wait_ge(s["y_ready"], m)
                V.tensor_tensor(samples(scaled[:]), samples(norm_bank(m, 1)[:]),
                                each(per_sample[:, 0, m * SB:(m + 1) * SB]), ALU.mult).then_inc(s["scaled1"], 1)

            def centre_time(m):
                dve.wait_ge(s["affine"], m + 1)
                own.link(V.tensor_reduce(sums[:], samples(t0[:]), AX.X, ALU.add))
                V.scalar_tensor_tensor(samples(t1[:]), each(sums[:]), -1.0 / S, samples(t0[:]), ALU.mult, ALU.add)\
                    .then_inc(s["time_centred"], 1)

            def var_time(m):
                dve.wait_ge(s["time_squared"], m + 1)
                own.link(V.tensor_reduce(rt[:], samples(sq[:]), AX.X, ALU.add))
                V.tensor_scalar(rt[:], rt[:], 1.0 / S, 1e-8, ALU.mult, ALU.add).then_inc(s["time_var"], 1)

            def film(m):
                dve.wait_ge(s["time_root"], m + 1)
                own.link(V.tensor_tensor(rt[:], rt[:], film_a[:, bass.ds(m * SB, SB)], ALU.mult))
                own.link(V.tensor_tensor(samples(t1[:]), samples(t1[:]), each(rt[:]), ALU.mult))
                if not (isinstance(m, int) and m == 0):
                    dve.wait_ge(s["h_low"], m)
                V.tensor_tensor(samples(hf[:]), samples(t1[:]), each(film_b[:, bass.ds(m * SB, SB)]), ALU.add)\
                    .then_inc(s["film_done"], 1)

            def router_max(m):
                logits = bank[6][:, 0:TB * E].rearrange("p (t e) -> p t e", e=E)
                dve.wait_ge(s["logits_mm"], m + 1)
                own.link(V.tensor_reduce(rmax[:], logits, AX.X, ALU.max))
                V.tensor_tensor(rprob[:], logits, perx(rmax[:]), ALU.subtract).then_inc(s["rmax_done"], 1)

            def router_pick(m):
                iota_e = iota_row[:, 0:E].unsqueeze(1).to_broadcast([P, TB, E])
                dve.wait_ge(s["exp_done"], m + 1)
                own.link(V.tensor_reduce(rv[:, 0, :], rprob[:], AX.X, ALU.add))
                own.link(V.reciprocal(rv[:, 1, :], rv[:, 0, :]))
                own.link(V.tensor_tensor(rprob[:], rprob[:], perx(rv[:, 1, :]), ALU.mult))
                own.link(V.tensor_reduce(rv[:, 2, :], rprob[:], AX.X, ALU.max))

                def pick(probs, largest, hot, number_):
                    own.link(V.tensor_tensor(hot, probs, perx(largest), ALU.is_equal))
                    own.link(V.scalar_tensor_tensor(hot, hot, -float(E), iota_e, ALU.mult, ALU.add))
                    own.link(V.tensor_reduce(number_, hot, AX.X, ALU.min))
                    own.link(V.tensor_tensor(hot, hot, perx(number_), ALU.is_equal))

                pick(rprob[:], rv[:, 2, :], rs[:, 0], rv[:, 3, :])
                own.link(V.scalar_tensor_tensor(rs[:, 1], rs[:, 0], -2.0, rprob[:], ALU.mult, ALU.add))
                own.link(V.tensor_reduce(rv[:, 4, :], rs[:, 1], AX.X, ALU.max))
                pick(rs[:, 1], rv[:, 4, :], rs[:, 2], rv[:, 3, :])
                own.mark(V.tensor_tensor(rv[:, 5, :], rv[:, 2, :], rv[:, 4, :], ALU.add))
                own.link(V.tensor_tensor(rs[:, 3], rs[:, 0], rs[:, 2], ALU.add))
                own.mark(V.reciprocal(rv[:, 1, :], rv[:, 5, :]))
                own.link(V.tensor_tensor(rs[:, 3], rs[:, 3], rprob[:], ALU.mult))
                V.tensor_tensor(comb[:], rs[:, 3], perx(rv[:, 1, :]), ALU.mult).then_inc(s["comb_ready"], 1)

            def copy_gates(m, first):
                dve.wait_ge(s["comb_mm"], m + 1)
                if not first:
                    dve.wait_ge(s["gates_stored"], 16 * m)
                    dve.wait_ge(s["bias_mm"], m)
                V.tensor_copy(comb_t[:], bank[7][0:E, :]).then_inc(s["comb_copied"], 1)

            def init_total(b, first):
                dve.wait_ge(s["bias_mm"], b + 1)
                if not first:
                    dve.wait_ge(s["out_turned"], b)
                V.tensor_tensor(total[:], bank[3][:], res[:, bass.ds(b * C, C)], ALU.add).then_inc(s["total_init"], 1)

            def low_hidden(b, n):
                m = n % 4
                dve.wait_ge(s["relu_done"], L * b + n + 1)
                if high_on_act(n):
                    dve.wait_ge(s["relu_high"], ACT_HIGHS * b + highs_by_act(n))
                else:
                    V.tensor_copy(act_h[:, m, :], act_f[:, m, :]).then_inc(s["relu_high_v"], 1)
                    dve.wait_ge(s["relu_high_v"], DVE_HIGHS * b + highs_by_dve(n))
                V.tensor_tensor(act_l[:, m, :], act_f[:, m, :], act_h[:, m, :], ALU.subtract).then_inc(s["relu_low"], 1)

            def weigh(b, e, fresh=False):
                dve.wait_ge(s["down_mm"], L * b + FT * (e + 1))
                dve.wait_ge(gates_loaded[2 * e // E], 16 * (b + 1))
                if not (fresh and e < 2):
                    dve.wait_ge(s["added"], E * b + e - 1)
                V.tensor_tensor(weighted[:, e % 2, :], down_bank[e % 2][:], gates[:, e, :], ALU.mult)\
                    .then_inc(s["weighted_done"], 1)

            own_first = Chain(dve, s["dve_first"])

            def experts(b, first, last):
                for n in range(L):
                    low_hidden(b, n)
                    if n == 0 and not first:
                        weigh(b - 1, E - 2)
                    if n == 4:
                        if not first:
                            weigh(b - 1, E - 1)
                        copy_gates(b, first)
                    if n >= 8 and n % FT == 0:
                        weigh(b, n // FT - 2, first)
                    if n == 8:
                        init_total(b, first)
                    if first:
                        if n == 13:
                            moments_of(NB - 1, 1, own_first)
                        if n == 17:
                            normalise(NB - 1, 1)
                        if n == 21:
                            scale_gamma(NB - 1)
                    if not last:
                        if n == 8:
                            moments_of(b + 1, 2)
                        if n == 11:
                            normalise(b + 1, 2)
                        if n == 16:
                            centre_time(b + 1)
                        if n == 19:
                            var_time(b + 1)
                        if n == 24:
                            film(b + 1)
                        if n == 28:
                            router_max(b + 1)
                        if n == 31:
                            router_pick(b + 1)

            x_block(0)
            low_in(0)
            low_in(1)
            low_out(0)
            x_block(1)
            low_out(1)
            dve.wait_ge(s["pads"], 3)
            dve.wait_ge(s["table_ready"], 1)
            for j in range(STEPS):
                k, half = divmod(j, 2)
                if j == 2:
                    x_block(2)
                if j == 6:
                    x_block(3)
                split(j)
                if half == 1 and k + 2 < NW and not in_on_pool(k + 2):
                    low_in(k + 2)
                if half == 0 and k >= 2:
                    finish(k - 2)
                if j == 8:
                    dve.wait_ge(s["style_out"], 8)
                    own.link(V.tensor_tensor(film_a[:], soft[:, 0, :], soft[:, 1, :], ALU.add))
                    V.tensor_scalar(film_a[:], film_a[:], 1e-8, None, ALU.add).then_inc(s["film_a_ready"], 1)
                if j == 22:
                    moments_of(0, 1)
                if j == 24:
                    normalise(0, 1)
                if j == 26:
                    scale_gamma(0)
                if j == 27:
                    moments_of(1, 1)
                if j == 29:
                    moments_of(0, 2)
            finish(NW - 2)
            normalise(1, 1)
            normalise(0, 2)
            finish(NW - 1)
            scale_gamma(1)
            centre_time(0)
            moments_of(2, 1)
            var_time(0)
            normalise(2, 1)
            film(0)
            scale_gamma(2)
            router_max(0)
            router_pick(0)
            before = own.count
            experts(0, True, False)
            per = own.count - before
            with dve.Fori(1, NB - 1) as b:
                own.enter(b - 1, per)
                experts(b, False, False)
            own.leave(NB - 2)
            experts(NB - 1, False, True)
            weigh(NB - 1, E - 2)
            weigh(NB - 1, E - 1)

        @block.scalar
        def _(act):
            A = nc.scalar
            def layer(n, dst, src, func, bias):
                act.wait_ge(s["style_mm"], n + 1)
                A.activation(dst, src, func, bias=bias).then_inc(s["style_out"], 1)

            for dst, src in ((emb[:], subj_emb), (gbb_r[:, 0, :], gamma), (gbb_r[:, 1, :], beta), (gbb_r[:, 2, :], bo),
                             (hw1[:], hyp_w1), (bi_r[:], bi), (hw2[:], hyp_w2), (sw1[:], sty_w1), (sw2[:], sty_w2),
                             (cols[:, HB1:HB1 + 1], col(hyp_b1)), (cols[:, HB2:HB2 + 1], col(hyp_b2)),
                             (cols[0:SH2, SB1:SB1 + 1], col(sty_b1)), (cols[:, SG:SG + 1], col(sty_b2[0:D])),
                             (cols[:, SBT:SBT + 1], col(sty_b2[D:2 * D]))):
                act.dma_start(dst, src).then_inc(s["params"], 16)

            def x_high(j):
                act.wait_ge(s["x_turned"], j + 1)
                A.copy(xh[:, j * C:(j + 1) * C], bank[6 + j % 2][:]).then_inc(s["x_high"], 1)

            def high_in(k):
                if k >= 2:
                    act.wait_ge(s["hid_mm"], 2 * k - 2)
                act.wait_ge(wi_landed[k % 2], 16 * (k // 2 + 1))
                A.copy(wih[:, k % 2, :], wraw[:, k % 2, 0:FF]).then_inc(s["wi_high"], 1)

            def high_out(k):
                if k >= 3:
                    act.wait_ge(s["out_mm"], 2 * k - 4)
                act.wait_ge(wo_landed[k % 2], 16 * (k // 2 + 1))
                A.copy(woh[:, k % 3, :], wraw[:, k % 2, FF:]).then_inc(s["wo_high"], 1)

            def gelu(j):
                k, half = divmod(j, 2)
                act.wait_ge(s["hid_mm"], j + 1)
                if j >= 4:
                    act.wait_ge(s["out_mm"], j - 3)
                for i in range(2):
                    A.activation(act_f[:, j % 4, i * CW:(i + 1) * CW], bank[j % 4][:, i * CW:(i + 1) * CW], ACT.Gelu,
                                 bias=bi_c[:, 2 * half + i, k:k + 1]).then_inc(s["gelu_done"], 1)

            act.wait_ge(s["small_mm"], 1)
            A.copy(sorted_expert[:], bank[1][0:E, 0:NS]).then_inc(s["small_out"], 1)
            A.copy(sorted_subject[:], bank[1][0:NU, NS:2 * NS]).then_inc(s["small_out"], 1)
            act.wait_ge(s["small_mm"], 2)
            A.copy(per_sample[:], bank[2][:, 0:3 * NS].rearrange("p (a n) -> p a n", a=3)).then_inc(s["small_out"], 1)

            act.wait_ge(s["params"], 14 * 16)
            act.wait_ge(s["style_mm"], 1)
            A.copy(se_t[:], bank[7][0:SE, 0:NS]).then_inc(s["style_out"], 1)
            layer(1, hyp_t[:], bank[7][:, NS:2 * NS], ACT.Relu, cols[:, HB1:HB1 + 1])
            layer(2, hyp2_t[:], bank[7][:, 2 * NS:3 * NS], ACT.Identity, cols[:, HB2:HB2 + 1])
            layer(3, sty_t[:], bank[7][0:SH2, 3 * NS:4 * NS], ACT.Relu, cols[0:SH2, SB1:SB1 + 1])
            layer(4, soft[:, 2, :], bank[7][:, 4 * NS:5 * NS], ACT.Abs, cols[:, SG:SG + 1])
            A.activation(soft[:, 0, :], bank[7][:, 4 * NS:5 * NS], ACT.Relu, bias=cols[:, SG:SG + 1])\
                .then_inc(s["style_out"], 1)
            A.activation(film_b[:], bank[7][:, 5 * NS:6 * NS], ACT.Identity, bias=cols[:, SBT:SBT + 1])\
                .then_inc(s["style_out"], 1)
            act.wait_ge(s["style_out"], 7)
            A.activation(soft[:, 2, :], soft[:, 2, :], ACT.Exp, scale=-1.0).then_inc(s["act_own"], 1)
            act.wait_ge(s["act_own"], 1)
            A.activation(soft[:, 1, :], soft[:, 2, :], ACT.Ln, bias=1.0).then_inc(s["style_out"], 1)

            act.wait_ge(s["small_mm"], 3)
            A.copy(bi_c[:], bank[3][:, 0:FT * NW].rearrange("p (a n) -> p a n", a=FT)).then_inc(s["small_out"], 1)
            A.copy(b1_c[:], bank[4][:, 0:FT * E].rearrange("p (a n) -> p a n", a=FT)).then_inc(s["small_out"], 1)
            act.wait_ge(s["small_out"], 5)

            def high_v(e):
                par = (e + 1) % 2
                landed = 16 * ((NW + 1 - par) // 2 + e // 2 + 1)
                act.wait_ge(wi_landed[par], landed)
                act.wait_ge(wo_landed[par], landed)
                A.copy(vh[:, e, :], wraw[:, par, :]).then_inc(s["v_high"], 1)

            def fetch_res(m):
                act.wait_ge(s["win_done"], whole(m))
                if m:
                    act.wait_ge(s["res_turned"], m)
                A.copy(fetched_res[:], res[:, m * C:(m + 1) * C]).then_inc(s["res_fetched"], 1)

            def fetch_y(m):
                act.wait_ge(s["y_ready"], m + 1)
                if not (isinstance(m, int) and m == 0):
                    act.wait_ge(s["y_turned"], m)
                A.copy(fetched_y[:], res[:, bass.ds(m * C, C)]).then_inc(s["fetched"], 1)

            def affine(m):
                act.wait_ge(s["back2"], m + 1)
                A.activation(t0[:], bank[6][:], ACT.Identity, bias=cols[:, LB:LB + 1], scale=cols[:, LG:LG + 1])\
                    .then_inc(s["affine"], 1)

            def square_time(m):
                act.wait_ge(s["time_centred"], m + 1)
                A.activation(sq[:], t1[:], ACT.Square).then_inc(s["time_squared"], 1)

            def high_tokens(m):
                act.wait_ge(s["film_done"], m + 1)
                A.copy(hh[:, bass.ds(m * C, C)], hf[:]).then_inc(s["h_high"], 1)

            def exp_router(m):
                act.wait_ge(s["rmax_done"], m + 1)
                A.activation(rprob[:], rprob[:], ACT.Exp).then_inc(s["exp_done"], 1)

            def copy_out(b, first):
                act.wait_ge(s["out_turned"], b + 1)
                if not first:
                    act.wait_ge(s["stored"], 16 * TB * b)
                A.copy(out_sb, bank[7][:].rearrange("p (t d) -> p t d", t=TB)).then_inc(s["out_copied"], 1)

            def relu(b, n, fresh):
                e, ft = divmod(n, FT)
                m = n % 4
                act.wait_ge(s["up_mm"], L * b + n + 1)
                if not (fresh and n < 4):
                    act.wait_ge(s["down_mm"], L * b + n - 3)
                A.activation(act_f[:, m, :], up_bank[n % 3][:], ACT.Relu, bias=b1_c[:, ft, e:e + 1])\
                    .then_inc(s["relu_done"], 1)
                if high_on_act(n):
                    A.activation(act_h[:, m, :], up_bank[n % 3][:], ACT.Relu, bias=b1_c[:, ft, e:e + 1])\
                        .then_inc(s["relu_high"], 1)

            def experts(b, first, last):
                for n in range(L):
                    relu(b, n, first)
                    if first and n % FT == 1 and n // FT + 2 < E:
                        high_v(n // FT + 2)
                    if n == 9 and not first:
                        copy_out(b - 1, isinstance(b, int) and b == 1)
                    if not last:
                        if n == 5:
                            fetch_y(b + 1)
                        if n == 15:
                            affine(b + 1)
                        if n == 18:
                            square_time(b + 1)
                        if n == 26:
                            high_tokens(b + 1)
                        if n == 30:
                            exp_router(b + 1)
                    if first and n == 10:
                        fetch_res(NB - 1)

            x_high(0)
            high_in(0)
            high_out(0)
            high_in(1)
            x_high(1)
            high_out(1)
            for j in range(STEPS):
                k, half = divmod(j, 2)
                if j == 2:
                    x_high(2)
                if j == 6:
                    x_high(3)
                gelu(j)
                if half == 1 and k + 2 < NW:
                    high_in(k + 2)
                if half == 0 and 1 <= k < NW - 1:
                    high_out(k + 1)
                if j == 21:
                    fetch_res(0)
                if j == 26:
                    fetch_res(1)
                if j == 28:
                    fetch_y(0)
            high_v(0)
            fetch_res(2)
            affine(0)
            square_time(0)
            high_v(1)
            high_tokens(0)
            exp_router(0)
            experts(0, True, False)
            with act.Fori(1, NB - 1) as b:
                experts(b, False, False)
            experts(NB - 1, False, True)
            copy_out(NB - 1, False)

        @block.tensor
        def _(pe):
            T = nc.tensor
            mm = T.matmul

            pe.wait_ge(s["consts2"], 1)
            pe.wait_ge(s["perm_ready"], 1)
            for q in range(SPT):
                last = mm(bank[0][:, 0:TT], part_of_quarter[:, q, :],
                          perm[:].rearrange("p (t q) -> p q t", q=SPT)[:, q, :], start=(q == 0), stop=(q == SPT - 1))
            last.then_inc(s["idx_mm"], 1)
            pe.wait_ge(s["perm_ready"], 3)
            mm(bank[1][0:E, 0:NS], hot_expert[:], perm[:], start=True, stop=True)
            mm(bank[1][0:NU, NS:2 * NS], hot_subject[:], perm[:], start=True, stop=True).then_inc(s["small_mm"], 1)
            pe.wait_ge(s["params"], 14 * 16)
            pe.wait_ge(s["small_out"], 2)
            for a in range(3):
                last = mm(bank[2][:, a * NS:(a + 1) * NS], gbb_r[:, a, :], sorted_expert[:], start=True, stop=True)
            last.then_inc(s["small_mm"], 1)

            def style(n, lhs, rhs, rows):
                if n:
                    pe.wait_ge(s["style_out"], n)
                mm(bank[7][0:rows, n * NS:(n + 1) * NS], lhs, rhs, start=True, stop=True).then_inc(s["style_mm"], 1)

            style(0, emb[:], sorted_subject[:], SE)
            style(1, hw1[:], se_t[:], SH)
            style(2, hw2[:], hyp_t[:], SH)
            style(3, sw1[:], hyp2_t[:], SH2)
            pe.wait_ge(s["style_out"], 4)
            mm(bank[7][:, 4 * NS:5 * NS], sw2[:, 0:D], sty_t[:], start=True, stop=True)
            mm(bank[7][:, 5 * NS:6 * NS], sw2[:, D:2 * D], sty_t[:], start=True, stop=True).then_inc(s["style_mm"], 1)

            pe.wait_ge(s["hot_ready"], 1)
            for ft in range(FT):
                mm(bank[3][:, ft * NW:(ft + 1) * NW], bi_r[:, ft * P:(ft + 1) * P], win_hot_t[:], start=True, stop=True)
            pe.wait_ge(s["params_late"], 5 * 16)
            for ft in range(FT):
                last = T.transpose(bank[4][:, ft * E:(ft + 1) * E], b1_r[:, ft * P:(ft + 1) * P], ident[0:E, 0:E])
            last.then_inc(s["small_mm"], 1)

            def turn_x(j):
                pe.wait_ge(gathered[j], 16 * TB)
                if j >= 2:
                    pe.wait_ge(s["x_read"], j - 1)
                if j == 1:
                    pe.wait_ge(s["style_out"], 7)
                for t in range(TB):
                    last = T.transpose(bank[6 + j % 2][:, t * P:(t + 1) * P], xg[:, j * TB + t, :], ident[:])
                last.then_inc(s["x_turned"], 1)

            starts = {}

            def up(j):
                k, half = divmod(j, 2)
                if half == 0:
                    starts[k] = pe.value_load(table[0:1, 1, k:k + 1], min_val=0, max_val=N)
                    pe.wait_ge(s["x_ready"], min(NB, ((k + 1) * G + SB - 1) // SB))
                    pe.wait_ge(s["wi_high"], k + 1)
                    pe.wait_ge(*low_of(k, "in"))
                if j >= 4:
                    pe.wait_ge(s["gelu_done"], 2 * (j - 3))
                if j in (3, 0):
                    pe.wait_ge(s["small_out"], 5)
                for i in range(2):
                    ft = 2 * half + i
                    dst = bank[j % 4][:, i * CW:(i + 1) * CW]
                    h, l = (v[:, k % 2, ft * P:(ft + 1) * P] for v in (wih, wil))
                    th, tl = (v[:, bass.ds(starts[k], CW)] for v in (xh, xl))
                    mm(dst, h, th, start=True, stop=False)
                    mm(dst, h, tl, start=False, stop=False)
                    last = mm(dst, l, th, start=False, stop=True)
                last.then_inc(s["hid_mm"], 1)

            def down(j):
                k, half = divmod(j, 2)
                if half == 0:
                    pe.wait_ge(s["wo_high"], k + 1)
                    pe.wait_ge(*low_of(k, "out"))
                    if k >= 2:
                        pe.wait_ge(s["win_done"], k - 1)
                pe.wait_ge(s["split_high"], j + 1)
                dst = down_bank[k % 2][:, 0:CW]
                for i in range(2):
                    ft = 2 * half + i
                    h, l = (v[:, k % 3, ft * P:(ft + 1) * P] for v in (woh, wol))
                    ah = act_h[:, j % 4, i * CW:(i + 1) * CW]
                    mm(dst, h, ah, start=(ft == 0), stop=False)
                    mm(dst, l, ah, start=False, stop=False)
                pe.wait_ge(s["split_low"], j + 1)
                for i in range(2):
                    ft = 2 * half + i
                    al = act_l[:, j % 4, i * CW:(i + 1) * CW]
                    last = mm(dst, woh[:, k % 3, ft * P:(ft + 1) * P], al, start=False, stop=(ft == FT - 1))
                last.then_inc(s["out_mm"], 1)

            def turn_res(m):
                pe.wait_ge(s["res_fetched"], m + 1)
                if m < 2:
                    pe.wait_ge(s["x_read"], m + 3)
                elif m == 2:
                    pe.wait_ge(s["gelu_done"], 2 * STEPS)
                else:
                    pe.wait_ge(s["total_init"], 1)
                for t in range(TB):
                    last = T.transpose(bank[norm1_bank[m]][:, t * P:(t + 1) * P], fetched_res[:, t * P:(t + 1) * P], ident[:])
                last.then_inc(s["res_turned"], 1)

            def turn_y(m):
                pe.wait_ge(s["fetched"], m + 1)
                if isinstance(m, int) and m == 0:
                    pe.wait_ge(s["scaled1"], 1)
                else:
                    pe.wait_ge(s["rmax_done"], m)
                for t in range(TB):
                    last = T.transpose(bank[6][:, t * P:(t + 1) * P], fetched_y[:, t * P:(t + 1) * P], ident[:])
                last.then_inc(s["y_turned"], 1)

            def turn_back(m, norm):
                dst = bank[6 if norm == 2 else norm1_bank[m]]
                pe.wait_ge(s[f"normed{norm}"], m + 1)
                for t in range(TB):
                    last = T.transpose(dst[:, t * P:(t + 1) * P], normal[norm - 1][:, t, :], ident[:])
                last.then_inc(s[f"back{norm}"], 1)

            def route(m):
                pe.wait_ge(s["film_done"], m + 1)
                for t in range(TB):
                    last = mm(bank[6][:, t * E:(t + 1) * E], hf[:, t * P:(t + 1) * P], rw[:], start=True, stop=True)
                last.then_inc(s["logits_mm"], 1)

            def turn_gates(m):
                pe.wait_ge(s["comb_ready"], m + 1)
                pe.wait_ge(s["scaled1"], 2)
                for t in range(TB):
                    last = T.transpose(bank[7][0:E, t * P:(t + 1) * P], comb[:, t, :], ident[:])
                last.then_inc(s["comb_mm"], 1)

            def bias_out(m, first):
                pe.wait_ge(s["comb_copied"], m + 1)
                if first:
                    pe.wait_ge(s["params_late"], 5 * 16)
                    pe.wait_ge(s["scaled1"], NB - 1)
                else:
                    pe.wait_ge(s["scaled1"], NB)
                    pe.wait_ge(s["total_init"], m)
                mm(bank[3][:], b2_r[:], comb_t[:], start=True, stop=True).then_inc(s["bias_mm"], 1)

            def up_v(b, n, fresh=False):
                e, ft = divmod(n, FT)
                if n == 0:
                    pe.wait_ge(s["h_low"], b + 1)
                if fresh:
                    pe.wait_ge(s["v_low"], e + 1)
                    if n < 3:
                        pe.wait_ge(s["gelu_done"], 2 * STEPS)
                before = n - 3 if n >= 3 else (30, 31, 29)[n] - L
                if not (fresh and n < 3):
                    pe.wait_ge(s["relu_done"], L * b + before + 1)
                    if before % L in [i for i in range(L) if high_on_act(i)]:
                        turns = highs_by_act(before) if before >= 0 else highs_by_act(before + L) - ACT_HIGHS
                        pe.wait_ge(s["relu_high"], ACT_HIGHS * b + turns)
                h, l = (v[:, e, ft * P:(ft + 1) * P] for v in (vh, vl))
                th, tl = (v[:, bass.ds(b * C, C)] for v in (hh, hl))
                mm(up_bank[n % 3][:], h, th, start=True, stop=False)
                mm(up_bank[n % 3][:], h, tl, start=False, stop=False)
                mm(up_bank[n % 3][:], l, th, start=False, stop=True).then_inc(s["up_mm"], 1)

            def down_v(b, n, fresh):
                e, ft = divmod(n, FT)
                if ft == 0 and not (fresh and e < 2):
                    pe.wait_ge(s["weighted_done"], E * b + e - 1)
                if high_on_act(n):
                    pe.wait_ge(s["relu_high"], ACT_HIGHS * b + highs_by_act(n))
                else:
                    pe.wait_ge(s["relu_high_v"], DVE_HIGHS * b + highs_by_dve(n))
                h, l = (v[:, e, FF + ft * P:FF + (ft + 1) * P] for v in (vh, vl))
                dst, m = down_bank[e % 2][:], n % 4
                mm(dst, h, act_h[:, m, :], start=(ft == 0), stop=False)
                mm(dst, l, act_h[:, m, :], start=False, stop=False)
                pe.wait_ge(s["relu_low"], L * b + n + 1)
                mm(dst, h, act_l[:, m, :], start=False, stop=(ft == FT - 1)).then_inc(s["down_mm"], 1)

            def turn_total(b):
                pe.wait_ge(s["added"], E * (b + 1))
                if not (isinstance(b, int) and b == NB - 1):
                    pe.wait_ge(s["comb_copied"], b + 2)
                for t in range(TB):
                    last = T.transpose(bank[7][:, t * P:(t + 1) * P], total[:, t * P:(t + 1) * P], ident[:])
                last.then_inc(s["out_turned"], 1)

            def experts(b, first, last):
                for n in range(L):
                    if n + LAG < L:
                        up_v(b, n + LAG, first)
                    elif not last:
                        up_v(b + 1, n + LAG - L)
                    down_v(b, n, first)
                    if n == 1:
                        turn_gates(b)
                    if n == 3:
                        bias_out(b, first)
                    if n == 5 and not first:
                        turn_total(b - 1)
                    if not last:
                        if n == 4:
                            turn_y(b + 1)
                        if n == 11:
                            turn_back(b + 1, 2)
                        if n == 24:
                            route(b + 1)
                    if first:
                        if n == 9:
                            turn_res(NB - 1)
                        if n == 17:
                            turn_back(NB - 1, 1)
                    elif n == 12:
                        pe.wait_ge(s["out_copied"], b)

            turn_x(0)
            pe.wait_ge(s["pads"], 3)
            pe.wait_ge(s["table_ready"], 1)
            up(0)
            up(1)
            turn_x(1)
            up(2)
            for j in range(STEPS):
                if j == 0:
                    turn_x(2)
                if j == 4:
                    turn_x(3)
                if j + LAG < STEPS:
                    up(j + LAG)
                down(j)
                if j == 19:
                    turn_res(0)
                if j == 23:
                    turn_back(0, 1)
                if j == 24:
                    turn_res(1)
                if j == 26:
                    turn_y(0)
            turn_back(0, 2)
            turn_back(1, 1)
            turn_res(2)
            turn_back(2, 1)
            route(0)
            for n in range(LAG):
                up_v(0, n, True)
            experts(0, True, False)
            with pe.Fori(1, NB - 1) as b:
                experts(b, False, False)
            experts(NB - 1, False, True)
            turn_total(NB - 1)


_INS = ['x', 'itok_B_0_7', 'itok_B_6_14', 'L0_cond_Wi', 'L0_cond_bi', 'L0_cond_Wo', 'L0_cond_bo', 'L0_cond_gamma',
        'L0_cond_beta', 'L1_cond_ln_g', 'L1_cond_ln_b', 'L1_cond_subj_emb', 'L1_cond_hyp_w1', 'L1_cond_hyp_b1',
        'L1_cond_hyp_w2', 'L1_cond_hyp_b2', 'L1_cond_sty_w1', 'L1_cond_sty_b1', 'L1_cond_sty_w2', 'L1_cond_sty_b2',
        'L1_cond_router_w', 'L1_cond_exp_w1', 'L1_cond_exp_b1', 'L1_cond_exp_w2', 'L1_cond_exp_b2']


def kernel(**inputs):
    import numpy as _np
    import concourse.bacc as _bacc
    from concourse import mybir as _mybir
    from concourse.bass_utils import run_bass_kernel_spmd as _run

    nc = _bacc.Bacc("TRN2", target_bir_lowering=False, num_devices=1)
    arrays, args = {}, []
    for name in _INS:
        a = _np.ascontiguousarray(inputs[name])
        arrays[f"in_{name}_dram"] = a
        args.append(nc.dram_tensor(f"in_{name}_dram", a.shape, _mybir.dt.from_np(a.dtype), kind="ExternalInput").ap())
    args.append(nc.dram_tensor("out_0_dram", inputs["x"].shape, _mybir.dt.float32, kind="ExternalOutput").ap())
    build(nc, *args)
    r = _run(nc, [arrays], core_ids=[0])
    return r.results[0]["out_0_dram"]
```

```python
from contextlib import ExitStack

import concourse.bass as bass
from concourse import mybir

F32 = mybir.dt.float32
F32R = mybir.dt.float32r
I32 = mybir.dt.int32
ALU = mybir.AluOpType
ACT = mybir.ActivationFunctionType
AX = mybir.AxisListType

P = 128


class Chain:

    def __init__(self, engine, semaphore):
        self.engine, self.semaphore, self.count, self.extra = engine, semaphore, 0, 0

    def mark(self, instruction):
        self.count += 1
        instruction.then_inc(self.semaphore, 1)

    def link(self, instruction):
        self.mark(instruction)
        self.engine.wait_ge(self.semaphore, self.count + self.extra)

    def enter(self, i, per_turn):
        self.start, self.per_turn, self.extra = self.count, per_turn, i * per_turn

    def leave(self, turns):
        assert self.count - self.start == self.per_turn, (self.count - self.start, self.per_turn)
        self.count, self.extra = self.start + turns * self.per_turn, 0


def build(nc, x, expert_of, subject_of, Wi, bi, Wo, bo, gamma, beta, ln_g, ln_b, subj_emb, hyp_w1, hyp_b1,
          hyp_w2, hyp_b2, sty_w1, sty_b1, sty_w2, sty_b2, router_w, exp_w1, exp_b1, exp_w2, exp_b2, out):
    NS, S, D = x.shape
    E, _, FF = Wi.shape
    NU, SE = subj_emb.shape
    SH, SH2 = sty_w1.shape
    N = NS * S
    FT = FF // P
    TT = N // P
    SPT = P // S
    C = 512
    NB = N // C
    SB = C // S
    TB = C // P
    G = 8
    CW = G * S
    NW = (NS - E) // G + E
    assert D == P and NW % 3 == 0
    SLOTS = 4
    NP = N + CW

    x_rows = x.rearrange("s t d -> (s t) d")
    out_rows = out.rearrange("s t d -> (s t) d")
    gate_rows = nc.dram_tensor("gate_rows", [NB, E * C], F32, kind="Internal").ap()

    def col(v):
        return v.rearrange("(p o) -> p o", o=1)

    with ExitStack() as ctx:
        def sb(name, shape, dt=F32):
            return ctx.enter_context(nc.sbuf_tensor(name, shape, dt))

        def sem(name):
            return ctx.enter_context(nc.semaphore(name))

        bank = [ctx.enter_context(nc.psum_tensor(f"bank{i}", [P, 512], F32)) for i in range(8)]

        ident = sb("ident", [P, P])
        iota_row = sb("iota_row", [P, NS])
        iota_part = sb("iota_part", [P, 1])
        iota_diag = sb("iota_diag", [P, P])
        total = sb("total", [P, C])
        part_of_quarter = total[0:NS, :].rearrange("p (q n) -> p q n", q=SPT)
        minus_half = sb("minus_half", [P, SB])
        fetched_y = sb("fetched_y", [P, C])
        zero_cols = fetched_y[:, 0:CW]

        ids_all = sb("ids_all", [P, NS], I32)
        ids_col = sb("ids_col", [NS, 2], I32)
        key_all = sb("key_all", [P, NS])
        key_col = sb("key_col", [NS, 1])
        idf_all = sb("idf_all", [P, NS])
        idf_col = sb("idf_col", [NS, 2])
        smaller = sb("smaller", [NS, NS])
        place = sb("place", [NS, 1])
        perm = sb("perm", [NS, NS])
        below = sb("below", [P, E + 1, NS])
        out_sb = below[:].rearrange("p e n -> p (e n)")[:, 0:C].rearrange("p (t d) -> p t d", d=D)
        first_of = sb("first_of", [P, E + 1])
        number = sb("number", [P, E])
        steps_cmp = sb("steps_cmp", [P, E, G])
        windows = sb("windows", [P, E])
        upto_mask = sb("upto_mask", [P, E, E])
        upto_part = sb("upto_part", [P, E, E])
        windows_in = sb("windows_in", [P, E])
        base_val = sb("base_val", [P, E])
        win_cmp = sb("win_cmp", [P, NW, E])
        win_expert = sb("win_expert", [P, NW])
        win_hot = sb("win_hot", [P, NW, E])
        win_part = sb("win_part", [P, NW, E])
        win_start = sb("win_start", [P, NW])
        PACK, FIELD = 3, NS + 1
        packed = sb("packed", [P, NW // PACK])
        expert_table = sb("expert_table", [1, NW], I32)
        start_table = sb("start_table", [1, NW // PACK], I32)
        hot_expert = sb("hot_expert", [NS, E])
        hot_subject = sb("hot_subject", [NS, NU])
        win_hot_t = sb("win_hot_t", [E, NW])
        row_index = sb("row_index", [P, TT], I32)
        part_in_sample = sb("part_in_sample", [P, 1])
        sorted_expert = sb("sorted_expert", [E, NS])
        sorted_subject = sb("sorted_subject", [NU, NS])

        bi_r = sb("bi_r", [E, FF])
        b1_r = sb("b1_r", [E, FF])
        b2_r = sb("b2_r", [E, D])
        gbb_r = sb("gbb_r", [E, 3, D])
        cols = sb("cols", [P, 7])
        HB1, HB2, SB1, SG, SBT, LG, LB = range(7)
        emb = sb("emb", [NU, SE])
        hw1 = sb("hw1", [SE, SH])
        hw2 = sb("hw2", [SH, SH])
        sw1 = sb("sw1", [SH, SH2])
        sw2 = sb("sw2", [SH2, 2 * D])
        rw = sb("rw", [D, E])
        per_sample = sb("per_sample", [P, 3, NS])
        bi_c = sb("bi_c", [P, FT, NW])
        b1_c = sb("b1_c", [P, FT, E])
        se_t = sb("se_t", [SE, NS])
        hyp_t = sb("hyp_t", [SH, NS])
        hyp2_t = sb("hyp2_t", [SH, NS])
        sty_t = sb("sty_t", [SH2, NS])
        film_a = sb("film_a", [P, NS])
        film_b = sb("film_b", [P, NS])
        soft = sb("soft", [P, 3, NS])

        early = sb("early", [P, TT * D + NP])
        xg = early[:, 0:TT * D].rearrange("p (t d) -> p t d", d=D)
        xh = sb("xh", [P, NP], F32R)
        xl = sb("xl", [P, NP], F32R)
        xb = early[:, TT * D:]
        res = sb("res", [P, NP])
        wraw = sb("wraw", [P, SLOTS, 2 * FF])
        window_parts = sb("window_parts", [P, 4, 3, FF], F32R)
        wih, wil, woh, wol = (window_parts[:, i] for i in range(4))
        act_f = sb("act_f", [P, 4, C])
        act_h = sb("act_h", [P, 4, C], F32R)
        act_l = sb("act_l", [P, 4, C], F32R)

        vh = sb("vh", [P, E, 2 * FF], F32R)
        OWN = 2
        vl_first = sb("vl_first", [P, OWN, 2 * FF], F32R)
        vl_later = window_parts[:].rearrange("p a b f -> p (a b f)").rearrange("p (e f) -> p e f", f=2 * FF)
        assert E - OWN <= vl_later.shape[1]
        vl = [vl_first[:, e, :] if e < OWN else vl_later[:, e - OWN, :] for e in range(E)]
        fetched_res = sb("fetched_res", [P, C])
        scaled = sb("scaled", [P, C])
        t0 = sb("t0", [P, C])
        t1 = sb("t1", [P, C])
        sq = sb("sq", [P, C])
        hf = sb("hf", [P, C])
        weighted = sb("weighted", [P, 2, C])
        hh, hl = xh, xl
        stats = [sb(f"stats{i}", [P, TB, 6]) for i in (1, 2)]
        moments = [sb(f"moments{i}", [P, TB, 2]) for i in (1, 2)]
        spread = [sb(f"spread{i}", [P, TB]) for i in (1, 2)]
        normal = [sb(f"normal{i}", [P, TB, D]) for i in (1, 2)]
        scratch = sb("scratch", [P, 1])
        table_call = sb("table_call", [P, 1])
        carrier = sb("carrier", [P, 1])
        block_index = sb("block_index", [P, TB], I32)
        sums = sb("sums", [P, SB])
        rt = sb("rt", [P, SB])
        rmax = sb("rmax", [P, TB])
        rprob = sb("rprob", [P, TB, E])
        rs = sb("rs", [P, 4, TB, E])
        rv = sb("rv", [P, 6, TB])
        comb = sb("comb", [P, TB, E])
        comb_t = sb("comb_t", [E, C])
        gates = early[:, 0:E * C].rearrange("p (e c) -> p e c", e=E)

        names = """ids expert_id subject_id params params_gbb params_late consts consts2 pool_own dve_own dve_first act_own
            idx_mm idx_ready perm_ready hot_ready table_ready starts_ready small_mm small_out style_mm style_out
            x_turned x_high x_ready x_read pads
            wi_high wo_high wi_low wi_low_pool wo_low wo_low_pool hid_mm gelu_done split_high split_low out_mm win_done
            res_fetched res_turned var1_ready rstd1_ready normed1 back1 scaled1 y_ready
            fetched y_turned var2_ready rstd2_ready normed2 back2 affine time_centred time_squared time_var time_root
            film_done h_high h_low logits_mm rmax_done exp_done comb_ready comb_mm comb_copied gates_stored bias_mm
            v_high v_low total_init up_mm relu_done relu_low down_mm weighted_done added out_turned out_copied
            index_copied last_added last_turned last_copied stored"""
        s = {name: sem(name) for name in names.split()}
        gathered = [sem(f"gathered{j}") for j in range(NB)]
        wi_landed = [sem(f"wi_landed{i}") for i in range(SLOTS)]
        wo_landed = [sem(f"wo_landed{i}") for i in range(SLOTS)]
        PARTS = 4
        PART = E // PARTS
        gates_loaded = [sem(f"gates_loaded{i}") for i in range(PARTS)]
        block = ctx.enter_context(nc.Block())

        L = E * FT
        whole = lambda m: ((m + 1) * SB - E) // G + E
        norm1_bank = (6, 7, 3, 3)
        STEPS = 2 * NW
        LAG = 3
        in_on_pool = lambda k: k >= 3
        out_on_pool = lambda k: k >= 2
        up_bank = [bank[0], bank[1], bank[2]]
        down_bank = [bank[4], bank[5]]

        def in_landed(q):
            return wi_landed[q % SLOTS], 16 * (q // SLOTS + 1)

        def out_landed(q):
            return wo_landed[q % SLOTS], 16 * (q // SLOTS + 1)

        def load_words(engine):
            return [engine.value_load(start_table[0:1, i:i + 1], min_val=0, max_val=FIELD ** PACK - 1)
                    for i in range(NW // PACK)]

        def start_of(engine, words, k):
            return engine.snap(words[k // PACK] // FIELD ** (k % PACK) % FIELD * S, min_val=0, max_val=N)

        def low_of(k, which):
            names, pool_has = {"in": (("wi_low", "wi_low_pool"), in_on_pool),
                               "out": (("wo_low", "wo_low_pool"), out_on_pool)}[which]
            return s[names[pool_has(k)]], sum(pool_has(j) == pool_has(k) for j in range(k + 1))

        @block.sync
        def _(sp):
            sp.dma_start(ids_all[:], expert_of.partition_broadcast(P)).then_inc(s["ids"], 16)
            sp.dma_start(ids_col[:, 1:2], col(subject_of)).then_inc(s["subject_id"], 16)
            for dst, src in ((b1_r[:], exp_b1), (sw1[:], sty_w1), (sw2[:], sty_w2), (cols[:, SG:SG + 1], col(sty_b2[0:D])),
                             (cols[:, SBT:SBT + 1], col(sty_b2[D:2 * D])), (b2_r[:], exp_b2), (rw[:], router_w),
                             (cols[:, LG:LG + 1], col(ln_g)), (cols[:, LB:LB + 1], col(ln_b))):
                sp.dma_start(dst, src).then_inc(s["params_late"], 16)
            sp.wait_ge(s["table_ready"], 1)

            def slot_free(sp, q):
                if q >= SLOTS and q - SLOTS < NW:
                    sp.wait_ge(s["wi_high"], q - SLOTS + 1)
                    sp.wait_ge(*low_of(q - SLOTS, "in"))
                    sp.wait_ge(s["wo_high"], q - SLOTS + 1)
                    sp.wait_ge(*low_of(q - SLOTS, "out"))
                elif q >= SLOTS:
                    sp.wait_ge(s["v_high"], q - SLOTS - NW + 1)
                    sp.wait_ge(s["v_low"], q - SLOTS - NW + 1)

            for k in range(NW):
                slot = k % SLOTS
                e = sp.value_load(expert_table[0:1, k:k + 1], min_val=0, max_val=E - 1)
                slot_free(sp, k)
                sp.dma_start(wraw[:, slot, 0:FF], Wi[bass.ds(e, 1), :, :].rearrange("o p f -> p (o f)"))\
                    .then_inc(wi_landed[slot], 16)
                sp.dma_start(wraw[:, slot, FF:2 * FF].rearrange("p (t d) -> p t d", t=FT),
                             Wo[bass.ds(e, 1), :, :].rearrange("o (t p) d -> p (o t) d", p=P))\
                    .then_inc(wo_landed[slot], 16)

            def load_v(e):
                slot = (NW + e) % SLOTS
                slot_free(sp, NW + e)
                sp.dma_start(wraw[:, slot, 0:FF], exp_w1[e]).then_inc(wi_landed[slot], 16)
                sp.dma_start(wraw[:, slot, FF:2 * FF].rearrange("p (t d) -> p t d", t=FT),
                             exp_w2[e].rearrange("(t p) d -> p t d", p=P)).then_inc(wo_landed[slot], 16)

            def gates_trip(b):
                sp.wait_ge(s["comb_copied"], b + 1)
                sp.dma_start(gate_rows[b:b + 1, :].rearrange("o (e c) -> (o e) c", e=E), comb_t[:])\
                    .then_inc(s["gates_stored"], 16)
                sp.wait_ge(s["gates_stored"], 16 * (b + 1))
                for part in range(PARTS):
                    if b:
                        sp.wait_ge(s["weighted_done"], E * (b - 1) + PART * (part + 1))
                    w = PART * C
                    sp.dma_start(gates[:, part * PART:(part + 1) * PART, :].rearrange("p e c -> p (e c)"),
                                 gate_rows[b, part * w:(part + 1) * w].partition_broadcast(P))\
                        .then_inc(gates_loaded[part], 16)

            for e in range(E - 2):
                load_v(e)
            gates_trip(0)
            for e in range(E - 2, E):
                load_v(e)
            for b in range(1, NB):
                gates_trip(b)

        @block.gpsimd
        def _(pool):
            own = Chain(pool, s["pool_own"])
            nc.gpsimd.iota(iota_row[:], pattern=[[1, NS]], base=0, channel_multiplier=0,
                           allow_small_or_imprecise_dtypes=True).then_inc(s["consts"], 1)
            nc.gpsimd.iota(iota_part[:], pattern=[[1, 1]], base=0, channel_multiplier=1,
                           allow_small_or_imprecise_dtypes=True).then_inc(s["consts"], 1)
            nc.gpsimd.iota(iota_diag[:], pattern=[[1, P]], base=0, channel_multiplier=-1,
                           allow_small_or_imprecise_dtypes=True).then_inc(s["consts"], 1)
            nc.gpsimd.iota(upto_mask[:], pattern=[[1, E], [-1, E]], base=0, channel_multiplier=0,
                           allow_small_or_imprecise_dtypes=True).then_inc(s["consts"], 1)
            own.link(nc.gpsimd.memset(part_of_quarter, 0.0))
            for q in range(SPT):
                own.link(nc.gpsimd.iota(part_of_quarter[:, q, q * S:(q + 1) * S], pattern=[[0, S]], base=0,
                                        channel_multiplier=S, allow_small_or_imprecise_dtypes=True))
                own.link(nc.gpsimd.iota(part_in_sample[q * S:(q + 1) * S, :], pattern=[[1, 1]], base=0,
                                        channel_multiplier=1, allow_small_or_imprecise_dtypes=True))
            nc.gpsimd.memset(scratch[:], 0.0).then_inc(s["consts2"], 1)
            nc.gpsimd.memset(minus_half[:], -0.5)
            nc.gpsimd.memset(zero_cols, 0.0).then_inc(s["consts2"], 1)
            for i, src in enumerate((gamma, beta, bo)):
                pool.dma_start(gbb_r[:, i, :], src).then_inc(s["params_gbb"], 16)

            def gather(j):
                for t in range(j * TB, (j + 1) * TB):
                    pool.indirect_dma_start(xg[:, t, :], None, x_rows,
                                            bass.IndirectOffsetOnAxis(row_index[:, t:t + 1], 0)).then_inc(gathered[j], 16)

            def low_in(k):
                pool.wait_ge(s["hid_mm"], 2 * k - 4)
                pool.wait_ge(*in_landed(k))
                pool.wait_ge(s["wi_high"], k + 1)
                nc.gpsimd.tensor_tensor(wil[:, k % 3, :], wraw[:, k % SLOTS, 0:FF], wih[:, k % 3, :], ALU.subtract)\
                    .then_inc(s["wi_low_pool"], 1)

            def low_out(k):
                if k >= 3:
                    pool.wait_ge(s["out_mm"], 2 * k - 4)
                pool.wait_ge(*out_landed(k))
                pool.wait_ge(s["wo_high"], k + 1)
                nc.gpsimd.tensor_tensor(wol[:, k % 3, :], wraw[:, k % SLOTS, FF:], woh[:, k % 3, :], ALU.subtract)\
                    .then_inc(s["wo_low_pool"], 1)

            def root(m, norm):
                pool.wait_ge(s[f"var{norm}_ready"], m + 1)
                v = spread[norm - 1][:]
                nc.gpsimd.tensor_tensor(v, v, minus_half[:, 0:TB], ALU.pow).then_inc(s[f"rstd{norm}_ready"], 1)

            def root_time(m):
                pool.wait_ge(s["time_var"], m + 1)
                nc.gpsimd.tensor_tensor(rt[:], rt[:], minus_half[:], ALU.pow).then_inc(s["time_root"], 1)

            samples = lambda v: v.rearrange("p (a n) -> p a n", n=S)
            each = lambda v: v.unsqueeze(2).to_broadcast([P, SB, S])

            def add_beta(m):
                pool.wait_ge(s["scaled1"], m + 1)
                nc.gpsimd.tensor_tensor(samples(res[:, m * C:(m + 1) * C]), samples(scaled[:]),
                                        each(per_sample[:, 1, m * SB:(m + 1) * SB]), ALU.add).then_inc(s["y_ready"], 1)

            pool.wait_ge(s["idx_ready"], 1)
            for j in range(NB):
                gather(j)
            for k in range(NW):
                if in_on_pool(k):
                    low_in(k)
                if k >= 1 and out_on_pool(k - 1):
                    low_out(k - 1)
                if k == NW - 2:
                    root(0, 1)
            low_out(NW - 1)

            def low_v(e):
                pool.wait_ge(s["v_high"], e + 1)
                nc.gpsimd.tensor_tensor(vl[e], wraw[:, (NW + e) % SLOTS, :], vh[:, e, :], ALU.subtract)\
                    .then_inc(s["v_low"], 1)

            def low_tokens(m):
                pool.wait_ge(s["h_high"], m + 1)
                nc.gpsimd.tensor_tensor(hl[:, bass.ds(m * C, C)], hf[:], hh[:, bass.ds(m * C, C)], ALU.subtract)\
                    .then_inc(s["h_low"], 1)

            def add(b, e):
                pool.wait_ge(s["weighted_done"], E * b + e + 1)
                if e:
                    pool.wait_ge(s["added"], E * b + e)
                else:
                    pool.wait_ge(s["total_init"], b + 1)
                nc.gpsimd.tensor_tensor(total[:], total[:], weighted[:, e % 2, :], ALU.add).then_inc(s["added"], 1)

            def scatter(b):
                pool.wait_ge(s["out_copied"], b + 1)
                nc.gpsimd.tensor_copy(block_index[:], row_index[:, bass.ds(b * TB, TB)]).then_inc(s["index_copied"], 1)
                pool.wait_ge(s["index_copied"], b + 1)
                nc.gpsimd.tensor_tensor(scratch[:], scratch[:], scratch[:], ALU.add)
                for t in range(TB):
                    pool.indirect_dma_start(out_rows, bass.IndirectOffsetOnAxis(block_index[:, t:t + 1], 0),
                                            out_sb[:, t, :], None).then_inc(s["stored"], 16)

            def experts(b, first, last):
                if first:
                    low_v(2)
                    root(2, 1)
                    low_v(3)
                else:
                    add(b - 1, E - 2)
                    add(b - 1, E - 1)
                if not last:
                    root(b + 1, 2)
                if first:
                    add_beta(2)
                    low_v(4)
                else:
                    scatter(b - 1)
                for e in range(E - 2):
                    if first and e == 3:
                        low_v(6)
                    if e == 3 and not last:
                        low_tokens(b + 1)
                    add(b, e)
                    if first and e in (0, 3):
                        low_v({0: 5, 3: 7}[e])
                    if e == 1 and not last:
                        root_time(b + 1)
                    if first and e == 1:
                        root(3, 1)
                    if first and e == 4:
                        add_beta(3)

            add_beta(0)
            root(0, 2)
            low_v(0)
            root_time(0)
            root(1, 1)
            low_tokens(0)
            add_beta(1)
            low_v(1)
            experts(0, True, False)
            with pool.Fori(1, NB - 1) as b:
                experts(b, False, False)
            experts(NB - 1, False, True)
            add(NB - 1, E - 2)
            for half in range(2):
                pool.wait_ge(s["last_copied"], half + 1)
                for t in (TB // 2 * half, TB // 2 * half + 1):
                    rows = row_index[:, TT - TB + t:TT - TB + t + 1]
                    pool.indirect_dma_start(out_rows, bass.IndirectOffsetOnAxis(rows, 0), out_sb[:, t, :], None)\
                        .then_inc(s["stored"], 16)
            pool.wait_ge(s["stored"], 16 * TT)

        @block.vector
        def _(dve):
            own = Chain(dve, s["dve_own"])
            V = nc.vector

            dve.wait_ge(s["consts"], 4)
            dve.wait_ge(s["ids"], 16)
            dve.wait_ge(s["expert_id"], 16)
            own.mark(V.tensor_copy(idf_all[:], ids_all[:]))
            own.mark(V.tensor_scalar(ident[:], iota_diag[:], 0.0, None, ALU.is_equal))
            own.link(V.tensor_copy(idf_col[:, 0:1], ids_col[:, 0:1]))
            own.mark(V.scalar_tensor_tensor(key_all[:], idf_all[:], float(NS), iota_row[:], ALU.mult, ALU.add))
            own.link(V.scalar_tensor_tensor(key_col[:], idf_col[:, 0:1], float(NS), iota_part[0:NS, :], ALU.mult, ALU.add))
            own.link(V.tensor_scalar(smaller[:], key_all[0:NS, :], key_col[:, 0:1], None, ALU.is_lt))
            own.link(V.tensor_reduce(place[:], smaller[:], AX.X, ALU.add))
            V.tensor_scalar(perm[:], iota_row[0:NS, :], place[:, 0:1], None, ALU.is_equal).then_inc(s["perm_ready"], 1)
            V.tensor_scalar(hot_expert[:], iota_row[0:NS, 0:E], idf_col[:, 0:1], None, ALU.is_equal)\
                .then_inc(s["perm_ready"], 1)
            dve.wait_ge(s["subject_id"], 16)
            own.link(V.tensor_copy(idf_col[:, 1:2], ids_col[:, 1:2]))
            V.tensor_scalar(hot_subject[:], iota_row[0:NS, 0:NU], idf_col[:, 1:2], None, ALU.is_equal)\
                .then_inc(s["perm_ready"], 1)

            own.link(V.tensor_tensor(below[:], idf_all[:].unsqueeze(1).to_broadcast([P, E + 1, NS]),
                                     iota_row[:, 0:E + 1].unsqueeze(2).to_broadcast([P, E + 1, NS]), ALU.is_lt))
            own.link(V.tensor_reduce(first_of[:], below[:], AX.X, ALU.add))

            dve.wait_ge(s["idx_mm"], 1)
            V.tensor_scalar(row_index[:], bank[0][:, 0:TT], part_in_sample[:, 0:1], None, ALU.add)\
                .then_inc(s["idx_ready"], 1)

            own.link(V.tensor_tensor(number[:], first_of[:, 1:E + 1], first_of[:, 0:E], ALU.subtract))
            steps = iota_row[:, 0:NS].rearrange("p (a g) -> p g a", g=G)[:, 0, 0:G]
            own.link(V.tensor_tensor(steps_cmp[:], number[:].unsqueeze(2).to_broadcast([P, E, G]),
                                     steps.unsqueeze(1).to_broadcast([P, E, G]), ALU.is_gt))
            own.link(V.tensor_reduce(windows[:], steps_cmp[:], AX.X, ALU.add))
            own.link(V.tensor_scalar(upto_part[:], upto_mask[:], 0.0, None, ALU.is_ge))
            own.link(V.tensor_tensor(upto_part[:], upto_part[:], windows[:].unsqueeze(1).to_broadcast([P, E, E]), ALU.mult))
            own.link(V.tensor_reduce(windows_in[:], upto_part[:], AX.X, ALU.add))
            own.link(V.tensor_tensor(base_val[:], windows_in[:], windows[:], ALU.subtract))
            own.link(V.scalar_tensor_tensor(base_val[:], base_val[:], -float(G), first_of[:, 0:E], ALU.mult, ALU.add))
            own.link(V.tensor_tensor(win_cmp[:], windows_in[:].unsqueeze(1).to_broadcast([P, NW, E]),
                                     iota_row[:, 0:NW].unsqueeze(2).to_broadcast([P, NW, E]), ALU.is_le))
            own.link(V.tensor_reduce(win_expert[:], win_cmp[:], AX.X, ALU.add))
            own.link(V.tensor_scalar(win_expert[:], win_expert[:], float(E - 1), None, ALU.min))
            V.tensor_copy(expert_table[:], win_expert[0:1, :]).then_inc(s["table_ready"], 1)
            V.tensor_scalar(win_hot_t[:], win_expert[0:E, :], iota_part[0:E, 0:1], None, ALU.is_equal)\
                .then_inc(s["hot_ready"], 1)
            own.link(V.tensor_tensor(win_hot[:], iota_row[:, 0:E].unsqueeze(1).to_broadcast([P, NW, E]),
                                     win_expert[:].unsqueeze(2).to_broadcast([P, NW, E]), ALU.is_equal))
            own.link(V.tensor_tensor(win_part[:], win_hot[:], base_val[:].unsqueeze(1).to_broadcast([P, NW, E]), ALU.mult))
            own.link(V.tensor_reduce(win_start[:], win_part[:], AX.X, ALU.add))
            own.link(V.scalar_tensor_tensor(win_start[:], iota_row[:, 0:NW], float(G), win_start[:], ALU.mult, ALU.add))
            own.link(V.tensor_scalar(win_start[:], win_start[:], float(NS), None, ALU.min))
            fields = win_start[:].rearrange("p (w f) -> p f w", f=PACK)
            own.link(V.scalar_tensor_tensor(packed[:], fields[:, PACK - 1, :], float(FIELD), fields[:, PACK - 2, :],
                                            ALU.mult, ALU.add))
            for f in range(PACK - 3, -1, -1):
                own.link(V.scalar_tensor_tensor(packed[:], packed[:], float(FIELD), fields[:, f, :], ALU.mult, ALU.add))
            V.tensor_copy(start_table[:], packed[0:1, :]).then_inc(s["starts_ready"], 1)

            dve.wait_ge(s["consts2"], 2)
            for v in (xh[:], xl[:], xb):
                V.tensor_copy(v[:, N:NP], zero_cols).then_inc(s["pads"], 1)
            dve.wait_ge(s["starts_ready"], 1)

            def x_block(j):
                dve.wait_ge(s["x_high"], j + 1)
                bk = bank[6 + j % 2]
                V.tensor_tensor(xl[:, j * C:(j + 1) * C], bk[:], xh[:, j * C:(j + 1) * C], ALU.subtract)\
                    .then_inc(s["x_ready"], 1)
                if j == 0:
                    dve.wait_ge(s["small_out"], 3)
                V.tensor_tensor(xb[:, j * C:(j + 1) * C].rearrange("p (a n) -> p a n", n=S),
                                bk[:].rearrange("p (a n) -> p a n", n=S),
                                per_sample[:, 2, j * SB:(j + 1) * SB].unsqueeze(2).to_broadcast([P, SB, S]),
                                ALU.add).then_inc(s["x_read"], 1)

            def low_in(k):
                if k >= 3:
                    dve.wait_ge(s["hid_mm"], 2 * k - 4)
                dve.wait_ge(*in_landed(k))
                dve.wait_ge(s["wi_high"], k + 1)
                V.tensor_tensor(wil[:, k % 3, :], wraw[:, k % SLOTS, 0:FF], wih[:, k % 3, :], ALU.subtract)\
                    .then_inc(s["wi_low"], 1)

            def low_out(k):
                dve.wait_ge(*out_landed(k))
                dve.wait_ge(s["wo_high"], k + 1)
                V.tensor_tensor(wol[:, k % 3, :], wraw[:, k % SLOTS, FF:], woh[:, k % 3, :], ALU.subtract)\
                    .then_inc(s["wo_low"], 1)

            def split(j):
                dve.wait_ge(s["gelu_done"], 2 * (j + 1))
                a, h, l = (v[:, j % 4, :] for v in (act_f, act_h, act_l))
                V.tensor_copy(h, a).then_inc(s["split_high"], 1)
                dve.wait_ge(s["split_high"], j + 1)
                V.tensor_tensor(l, a, h, ALU.subtract).then_inc(s["split_low"], 1)

            def finish(k):
                start = start_of(dve, words, k)
                if k:
                    dve.wait_ge(s["win_done"], k)
                dve.wait_ge(s["out_mm"], 2 * (k + 1))
                V.tensor_tensor(res[:, bass.ds(start, CW)], down_bank[k % 2][:, 0:CW], xb[:, bass.ds(start, CW)], ALU.add)\
                    .then_inc(s["win_done"], 1)

            samples = lambda v: v.rearrange("p (a n) -> p a n", n=S)
            each = lambda v: v.unsqueeze(2).to_broadcast([P, SB, S])
            tiles = lambda v: v.rearrange("p (t d) -> p t d", t=TB)
            perx = lambda v: v.unsqueeze(2).to_broadcast([P, TB, E])

            def norm_bank(m, norm):
                return bank[6 if norm == 2 else norm1_bank[m]]

            def moments_of(m, norm, own=own):
                dve.wait_ge(s["res_turned" if norm == 1 else "y_turned"], m + 1)
                for t in range(TB):
                    own.mark(V.bn_stats(stats[norm - 1][:, t, :], tiles(norm_bank(m, norm)[:])[:, t, :]))
                dve.wait_ge(own.semaphore, own.count + own.extra)
                V.tensor_copy(carrier[:], iota_part[:])
                for t in range(TB):
                    own.mark(V.bn_aggr(moments[norm - 1][:, t, :], stats[norm - 1][:, t, :]))
                dve.wait_ge(own.semaphore, own.count + own.extra)
                V.tensor_scalar(spread[norm - 1][:], moments[norm - 1][:, :, 1], {1: 1e-12, 2: 1e-5}[norm], None, ALU.add)\
                    .then_inc(s[f"var{norm}_ready"], 1)

            def normalise(m, norm):
                dve.wait_ge(s[f"rstd{norm}_ready"], m + 1)
                if not (isinstance(m, int) and m == 0):
                    dve.wait_ge(s[f"back{norm}"], m)
                for t in range(TB):
                    ins = V.tensor_scalar(normal[norm - 1][:, t, :], tiles(norm_bank(m, norm)[:])[:, t, :],
                                          moments[norm - 1][:, t, 0:1], spread[norm - 1][:, t:t + 1],
                                          ALU.subtract, ALU.mult)
                ins.then_inc(s[f"normed{norm}"], 1)

            def scale_gamma(m):
                dve.wait_ge(s["back1"], m + 1)
                if m:
                    dve.wait_ge(s["y_ready"], m)
                V.tensor_tensor(samples(scaled[:]), samples(norm_bank(m, 1)[:]),
                                each(per_sample[:, 0, m * SB:(m + 1) * SB]), ALU.mult).then_inc(s["scaled1"], 1)

            def centre_time(m):
                dve.wait_ge(s["affine"], m + 1)
                own.link(V.tensor_reduce(sums[:], samples(t0[:]), AX.X, ALU.add))
                V.scalar_tensor_tensor(samples(t1[:]), each(sums[:]), -1.0 / S, samples(t0[:]), ALU.mult, ALU.add)\
                    .then_inc(s["time_centred"], 1)

            def var_time(m):
                dve.wait_ge(s["time_squared"], m + 1)
                own.link(V.tensor_reduce(rt[:], samples(sq[:]), AX.X, ALU.add))
                V.tensor_scalar(rt[:], rt[:], 1.0 / S, 1e-8, ALU.mult, ALU.add).then_inc(s["time_var"], 1)

            def film(m):
                dve.wait_ge(s["time_root"], m + 1)
                own.link(V.tensor_tensor(rt[:], rt[:], film_a[:, bass.ds(m * SB, SB)], ALU.mult))
                own.link(V.tensor_tensor(samples(t1[:]), samples(t1[:]), each(rt[:]), ALU.mult))
                if not (isinstance(m, int) and m == 0):
                    dve.wait_ge(s["h_low"], m)
                V.tensor_tensor(samples(hf[:]), samples(t1[:]), each(film_b[:, bass.ds(m * SB, SB)]), ALU.add)\
                    .then_inc(s["film_done"], 1)

            def router_max(m):
                logits = bank[6][:, 0:TB * E].rearrange("p (t e) -> p t e", e=E)
                dve.wait_ge(s["logits_mm"], m + 1)
                own.link(V.tensor_reduce(rmax[:], logits, AX.X, ALU.max))
                V.tensor_tensor(rprob[:], logits, perx(rmax[:]), ALU.subtract).then_inc(s["rmax_done"], 1)

            iota_e = iota_row[:, 0:E].unsqueeze(1).to_broadcast([P, TB, E])
            hot1, rest, hot2, both = (rs[:, i] for i in range(4))
            total_p, scale_p, largest1, number_p, largest2, pair = (rv[:, i, :] for i in range(6))

            def choose(own, probs, largest, hot):
                own.link(V.tensor_tensor(hot, probs, perx(largest), ALU.is_equal))
                own.link(V.scalar_tensor_tensor(hot, hot, -float(E), iota_e, ALU.mult, ALU.add))
                own.link(V.tensor_reduce(number_p, hot, AX.X, ALU.min))
                own.link(V.tensor_tensor(hot, hot, perx(number_p), ALU.is_equal))

            def router_probs(m, own=own):
                dve.wait_ge(s["exp_done"], m + 1)
                own.link(V.tensor_reduce(total_p, rprob[:], AX.X, ALU.add))
                own.link(V.reciprocal(scale_p, total_p))
                own.link(V.tensor_tensor(rprob[:], rprob[:], perx(scale_p), ALU.mult))
                own.link(V.tensor_reduce(largest1, rprob[:], AX.X, ALU.max))

            def router_first(m, own=own):
                choose(own, rprob[:], largest1, hot1)

            def router_second(m, own=own):
                own.link(V.scalar_tensor_tensor(rest, hot1, -2.0, rprob[:], ALU.mult, ALU.add))
                own.link(V.tensor_reduce(largest2, rest, AX.X, ALU.max))
                choose(own, rest, largest2, hot2)

            def router_gates(m, own=own):
                own.mark(V.tensor_tensor(pair, largest1, largest2, ALU.add))
                own.link(V.tensor_tensor(both, hot1, hot2, ALU.add))
                own.mark(V.reciprocal(scale_p, pair))
                own.link(V.tensor_tensor(both, both, rprob[:], ALU.mult))
                V.tensor_tensor(comb[:], both, perx(scale_p), ALU.mult).then_inc(s["comb_ready"], 1)

            def copy_gates(m, first):
                dve.wait_ge(s["comb_mm"], m + 1)
                if not first:
                    dve.wait_ge(s["gates_stored"], 16 * m)
                    dve.wait_ge(s["bias_mm"], m)
                V.tensor_copy(comb_t[:], bank[7][0:E, :]).then_inc(s["comb_copied"], 1)

            def init_total(b, first):
                dve.wait_ge(s["bias_mm"], b + 1)
                if not first:
                    dve.wait_ge(s["out_turned"], b)
                V.tensor_tensor(total[:], bank[3][:], res[:, bass.ds(b * C, C)], ALU.add).then_inc(s["total_init"], 1)

            def low_hidden(b, n):
                m = n % 4
                dve.wait_ge(s["relu_done"], 2 * (L * b + n + 1))
                V.tensor_tensor(act_l[:, m, :], act_f[:, m, :], act_h[:, m, :], ALU.subtract).then_inc(s["relu_low"], 1)

            def weigh(b, e, fresh=False):
                dve.wait_ge(s["down_mm"], L * b + FT * (e + 1))
                dve.wait_ge(gates_loaded[e // PART], 16 * (b + 1))
                if not (fresh and e < 2):
                    dve.wait_ge(s["added"], E * b + e - 1)
                V.tensor_tensor(weighted[:, e % 2, :], down_bank[e % 2][:], gates[:, e, :], ALU.mult)\
                    .then_inc(s["weighted_done"], 1)

            own_first = Chain(dve, s["dve_first"])

            def experts(b, first, last):
                for n in range(L):
                    low_hidden(b, n)
                    if n >= 8 and n % FT == 0:
                        weigh(b, n // FT - 2, first)
                    if n in (0, 4) and not first:
                        weigh(b - 1, E - 2 + n // FT)
                    if n == (12 if first else 10):
                        init_total(b, first)
                    if first and n == 0:
                        router_second(b, own_first)
                    if first and n == 1:
                        router_gates(b, own_first)
                    if n == (4 if first else 2):
                        copy_gates(b, first)
                    if first and n == 3:
                        moments_of(2, 1, own_first)
                    if first and n == 5:
                        normalise(2, 1)
                    if first and n == 8:
                        scale_gamma(2)
                    if first:
                        if n == 17:
                            moments_of(NB - 1, 1, own_first)
                        if n == 21:
                            normalise(NB - 1, 1)
                        if n == 25:
                            scale_gamma(NB - 1)
                    if not last:
                        if n == (6 if first else 5):
                            moments_of(b + 1, 2)
                        if n == (9 if first else 7):
                            normalise(b + 1, 2)
                        if n == (14 if first else 13):
                            centre_time(b + 1)
                        if n == 16:
                            var_time(b + 1)
                        if n == 19:
                            film(b + 1)
                        if n == 23:
                            router_max(b + 1)
                        if n == 26:
                            router_probs(b + 1)
                        if n == 27:
                            router_first(b + 1)
                        if n == 29:
                            router_second(b + 1)
                        if n == 30:
                            router_gates(b + 1)

            words = load_words(dve)
            low_in(0)
            x_block(0)
            low_out(0)
            low_in(1)
            low_out(1)
            finished = 0
            for j in range(STEPS):
                k, half = divmod(j, 2)
                if j == 2:
                    x_block(2)
                if j == 6:
                    x_block(3)
                split(j)
                if j == 0:
                    x_block(1)
                    low_in(2)
                if half == 1 and k + 3 < NW and not in_on_pool(k + 3):
                    low_in(k + 3)
                if j == 27:
                    moments_of(0, 2)
                if j == 28:
                    normalise(0, 2)
                due = (j - 3) // 2 if j >= 19 else (j - 4) // 2
                if due >= finished:
                    finish(finished)
                    finished += 1
                if j == 20:
                    moments_of(0, 1)
                if j == 22:
                    normalise(0, 1)
                if j == 25:
                    scale_gamma(0)
            assert finished == NW - 1
            centre_time(0)
            finish(NW - 1)
            dve.wait_ge(s["style_out"], 8)
            own.link(V.tensor_tensor(film_a[:], soft[:, 0, :], soft[:, 1, :], ALU.add))
            own.link(V.tensor_scalar(film_a[:], film_a[:], 1e-8, None, ALU.add))
            var_time(0)
            moments_of(1, 1)
            film(0)
            normalise(1, 1)
            router_max(0)
            scale_gamma(1)
            router_probs(0)
            router_first(0)
            before = own.count
            experts(0, True, False)
            per = own.count - before
            with dve.Fori(1, NB - 1) as b:
                own.enter(b - 1, per)
                experts(b, False, False)
            own.leave(NB - 2)
            experts(NB - 1, False, True)
            weigh(NB - 1, E - 2)
            dve.wait_ge(s["down_mm"], L * NB)
            dve.wait_ge(gates_loaded[PARTS - 1], 16 * NB)
            dve.wait_ge(s["added"], E * NB - 2)
            for half in range(2):
                c = slice(C // 2 * half, C // 2 * (half + 1))
                own.link(V.tensor_tensor(weighted[:, 1, c], down_bank[1][:, c], gates[:, E - 1, c], ALU.mult))
                if half == 0:
                    dve.wait_ge(s["added"], E * NB - 1)
                V.tensor_tensor(total[:, c], total[:, c], weighted[:, 1, c], ALU.add).then_inc(s["last_added"], 1)

        @block.scalar
        def _(act):
            A = nc.scalar
            def layer(n, dst, src, func, bias):
                act.wait_ge(s["style_mm"], n + 1)
                A.activation(dst, src, func, bias=bias).then_inc(s["style_out"], 1)

            act.dma_start(ids_col[:, 0:1], col(expert_of)).then_inc(s["expert_id"], 16)
            for dst, src in ((bi_r[:], bi), (emb[:], subj_emb), (hw1[:], hyp_w1), (hw2[:], hyp_w2),
                             (cols[:, HB1:HB1 + 1], col(hyp_b1)), (cols[:, HB2:HB2 + 1], col(hyp_b2)),
                             (cols[0:SH2, SB1:SB1 + 1], col(sty_b1))):
                act.dma_start(dst, src).then_inc(s["params"], 16)

            def x_high(j):
                act.wait_ge(s["x_turned"], j + 1)
                A.copy(xh[:, j * C:(j + 1) * C], bank[6 + j % 2][:]).then_inc(s["x_high"], 1)

            def high_in(k):
                if k >= 3:
                    act.wait_ge(s["hid_mm"], 2 * k - 4)
                act.wait_ge(*in_landed(k))
                A.copy(wih[:, k % 3, :], wraw[:, k % SLOTS, 0:FF]).then_inc(s["wi_high"], 1)

            def high_out(k):
                if k >= 3:
                    act.wait_ge(s["out_mm"], 2 * k - 4)
                act.wait_ge(*out_landed(k))
                A.copy(woh[:, k % 3, :], wraw[:, k % SLOTS, FF:]).then_inc(s["wo_high"], 1)

            def gelu(j):
                k, half = divmod(j, 2)
                act.wait_ge(s["hid_mm"], j + 1)
                if j >= 4:
                    act.wait_ge(s["out_mm"], j - 3)
                for i in range(2):
                    A.activation(act_f[:, j % 4, i * CW:(i + 1) * CW], bank[j % 4][:, i * CW:(i + 1) * CW], ACT.Gelu,
                                 bias=bi_c[:, 2 * half + i, k:k + 1]).then_inc(s["gelu_done"], 1)

            act.wait_ge(s["consts2"], 2)
            A.activation(table_call[:], minus_half[:, 0:1], ACT.Gelu)

            act.wait_ge(s["small_mm"], 1)
            A.copy(sorted_expert[:], bank[1][0:E, 0:NS]).then_inc(s["small_out"], 1)
            A.copy(sorted_subject[:], bank[1][0:NU, NS:2 * NS]).then_inc(s["small_out"], 1)
            act.wait_ge(s["small_mm"], 2)
            A.copy(per_sample[:], bank[2][:, 0:3 * NS].rearrange("p (a n) -> p a n", a=3)).then_inc(s["small_out"], 1)

            act.wait_ge(s["small_mm"], 3)
            A.copy(bi_c[:], bank[3][:, 0:FT * NW].rearrange("p (a n) -> p a n", a=FT)).then_inc(s["small_out"], 1)
            A.copy(b1_c[:], bank[4][:, 0:FT * E].rearrange("p (a n) -> p a n", a=FT)).then_inc(s["small_out"], 1)
            act.wait_ge(s["small_out"], 5)

            def softplus():
                act.wait_ge(s["style_out"], 7)
                A.activation(soft[:, 2, :], soft[:, 2, :], ACT.Exp, scale=-1.0).then_inc(s["act_own"], 1)
                act.wait_ge(s["act_own"], 1)
                A.activation(soft[:, 1, :], soft[:, 2, :], ACT.Ln, bias=1.0).then_inc(s["style_out"], 1)

            def high_v(e):
                act.wait_ge(*in_landed(NW + e))
                act.wait_ge(*out_landed(NW + e))
                A.copy(vh[:, e, :], wraw[:, (NW + e) % SLOTS, :]).then_inc(s["v_high"], 1)

            def fetch_res(m):
                act.wait_ge(s["win_done"], whole(m))
                if m:
                    act.wait_ge(s["res_turned"], m)
                A.copy(fetched_res[:], res[:, m * C:(m + 1) * C]).then_inc(s["res_fetched"], 1)

            def fetch_y(m):
                act.wait_ge(s["y_ready"], m + 1)
                if not (isinstance(m, int) and m == 0):
                    act.wait_ge(s["y_turned"], m)
                A.copy(fetched_y[:], res[:, bass.ds(m * C, C)]).then_inc(s["fetched"], 1)

            def affine(m):
                act.wait_ge(s["back2"], m + 1)
                A.activation(t0[:], bank[6][:], ACT.Identity, bias=cols[:, LB:LB + 1], scale=cols[:, LG:LG + 1])\
                    .then_inc(s["affine"], 1)

            def square_time(m):
                act.wait_ge(s["time_centred"], m + 1)
                A.activation(sq[:], t1[:], ACT.Square).then_inc(s["time_squared"], 1)

            def high_tokens(m):
                act.wait_ge(s["film_done"], m + 1)
                A.copy(hh[:, bass.ds(m * C, C)], hf[:]).then_inc(s["h_high"], 1)

            def exp_router(m):
                act.wait_ge(s["rmax_done"], m + 1)
                A.activation(rprob[:], rprob[:], ACT.Exp).then_inc(s["exp_done"], 1)

            def copy_out(b, first):
                act.wait_ge(s["out_turned"], b + 1)
                if not first:
                    act.wait_ge(s["stored"], 16 * TB * b)
                A.copy(out_sb, bank[7][:].rearrange("p (t d) -> p t d", t=TB)).then_inc(s["out_copied"], 1)

            def relu(b, n, fresh):
                e, ft = divmod(n, FT)
                m = n % 4
                act.wait_ge(s["up_mm"], L * b + n + 1)
                if not (fresh and n < 4):
                    act.wait_ge(s["down_mm"], L * b + n - 3)
                A.activation(act_f[:, m, :], up_bank[n % 3][:], ACT.Relu, bias=b1_c[:, ft, e:e + 1])\
                    .then_inc(s["relu_done"], 1)
                A.activation(act_h[:, m, :], up_bank[n % 3][:], ACT.Relu, bias=b1_c[:, ft, e:e + 1])\
                    .then_inc(s["relu_done"], 1)

            def experts(b, first, last):
                for n in range(L):
                    relu(b, n, first)
                    if first and n % FT == 1 and n // FT + 2 < E:
                        high_v(n // FT + 2)
                    if n == 10 and not first:
                        copy_out(b - 1, isinstance(b, int) and b == 1)
                    if not last:
                        if n == (1 if first else 0):
                            fetch_y(b + 1)
                        if n == (12 if first else 11):
                            affine(b + 1)
                        if n == 15:
                            square_time(b + 1)
                        if n == 21:
                            high_tokens(b + 1)
                        if n == 25:
                            exp_router(b + 1)
                    if first and n == 10:
                        fetch_res(NB - 1)

            act.wait_ge(s["params"], 7 * 16)
            act.wait_ge(s["params_late"], 9 * 16)
            act.wait_ge(s["style_mm"], 1)
            A.copy(se_t[:], bank[7][0:SE, 0:NS]).then_inc(s["style_out"], 1)
            high_in(0)
            layer(1, hyp_t[:], bank[7][:, NS:2 * NS], ACT.Relu, cols[:, HB1:HB1 + 1])
            x_high(0)
            layer(2, hyp2_t[:], bank[7][:, 2 * NS:3 * NS], ACT.Identity, cols[:, HB2:HB2 + 1])
            layer(3, sty_t[:], bank[7][0:SH2, 3 * NS:4 * NS], ACT.Relu, cols[0:SH2, SB1:SB1 + 1])
            high_out(0)
            layer(4, soft[:, 2, :], bank[7][:, 4 * NS:5 * NS], ACT.Abs, cols[:, SG:SG + 1])
            A.activation(soft[:, 0, :], bank[7][:, 4 * NS:5 * NS], ACT.Relu, bias=cols[:, SG:SG + 1])\
                .then_inc(s["style_out"], 1)
            A.activation(film_b[:], bank[7][:, 5 * NS:6 * NS], ACT.Identity, bias=cols[:, SBT:SBT + 1])\
                .then_inc(s["style_out"], 1)
            high_in(1)
            high_out(1)
            for j in range(STEPS):
                k, half = divmod(j, 2)
                if j == 2:
                    x_high(2)
                if j == 6:
                    x_high(3)
                gelu(j)
                if j == 0:
                    x_high(1)
                    high_in(2)
                if half == 1 and k + 3 < NW:
                    high_in(k + 3)
                if half == 0 and 1 <= k < NW - 1:
                    high_out(k + 1)
                if j == 20:
                    fetch_res(0)
                if j == 24:
                    fetch_res(1)
                if j == 26:
                    fetch_y(0)
            softplus()
            affine(0)
            high_v(0)
            square_time(0)
            A.activation(table_call[:], minus_half[:, 0:1], ACT.Exp)
            fetch_res(2)
            high_v(1)
            high_tokens(0)
            exp_router(0)
            experts(0, True, False)
            with act.Fori(1, NB - 1) as b:
                experts(b, False, False)
            experts(NB - 1, False, True)
            act.wait_ge(s["stored"], 16 * TB * (NB - 1))
            for half in range(2):
                act.wait_ge(s["last_turned"], half + 1)
                tiles = slice(TB // 2 * half, TB // 2 * (half + 1))
                A.copy(out_sb[:, tiles, :], bank[7 - half][:, 0:C // 2].rearrange("p (t d) -> p t d", t=TB // 2))\
                    .then_inc(s["last_copied"], 1)

        @block.tensor
        def _(pe):
            T = nc.tensor
            mm = T.matmul

            pe.wait_ge(s["consts2"], 1)
            pe.wait_ge(s["perm_ready"], 1)
            for q in range(SPT):
                last = mm(bank[0][:, 0:TT], part_of_quarter[:, q, :],
                          perm[:].rearrange("p (t q) -> p q t", q=SPT)[:, q, :], start=(q == 0), stop=(q == SPT - 1))
            last.then_inc(s["idx_mm"], 1)
            pe.wait_ge(s["perm_ready"], 3)
            mm(bank[1][0:E, 0:NS], hot_expert[:], perm[:], start=True, stop=True)
            mm(bank[1][0:NU, NS:2 * NS], hot_subject[:], perm[:], start=True, stop=True).then_inc(s["small_mm"], 1)
            pe.wait_ge(s["params_gbb"], 3 * 16)
            pe.wait_ge(s["small_out"], 2)
            for a in range(3):
                last = mm(bank[2][:, a * NS:(a + 1) * NS], gbb_r[:, a, :], sorted_expert[:], start=True, stop=True)
            last.then_inc(s["small_mm"], 1)

            pe.wait_ge(s["params"], 7 * 16)
            pe.wait_ge(s["hot_ready"], 1)
            for ft in range(FT):
                mm(bank[3][:, ft * NW:(ft + 1) * NW], bi_r[:, ft * P:(ft + 1) * P], win_hot_t[:], start=True, stop=True)
            pe.wait_ge(s["params_late"], 9 * 16)
            for ft in range(FT):
                last = T.transpose(bank[4][:, ft * E:(ft + 1) * E], b1_r[:, ft * P:(ft + 1) * P], ident[0:E, 0:E])
            last.then_inc(s["small_mm"], 1)

            def style(n, lhs, rhs, rows):
                if n:
                    pe.wait_ge(s["style_out"], n)
                mm(bank[7][0:rows, n * NS:(n + 1) * NS], lhs, rhs, start=True, stop=True).then_inc(s["style_mm"], 1)

            def turn_x(j):
                pe.wait_ge(gathered[j], 16 * TB)
                if j >= 2:
                    pe.wait_ge(s["x_read"], j - 1)
                if j == 1:
                    pe.wait_ge(s["style_out"], 7)
                for t in range(TB):
                    last = T.transpose(bank[6 + j % 2][:, t * P:(t + 1) * P], xg[:, j * TB + t, :], ident[:])
                last.then_inc(s["x_turned"], 1)

            start_at = {}

            def up(j):
                k, half = divmod(j, 2)
                if half == 0:
                    start_at[k] = start_of(pe, words, k)
                start = start_at[k]
                if half == 0:
                    pe.wait_ge(s["x_ready"], min(NB, ((k + 1) * G + SB - 1) // SB))
                    pe.wait_ge(s["wi_high"], k + 1)
                    pe.wait_ge(*low_of(k, "in"))
                if j >= 4:
                    pe.wait_ge(s["gelu_done"], 2 * (j - 3))
                if j in (3, 0):
                    pe.wait_ge(s["small_out"], 5)
                for i in range(2):
                    ft = 2 * half + i
                    dst = bank[j % 4][:, i * CW:(i + 1) * CW]
                    h, l = (v[:, k % 3, ft * P:(ft + 1) * P] for v in (wih, wil))
                    th, tl = (v[:, bass.ds(start, CW)] for v in (xh, xl))
                    mm(dst, h, th, start=True, stop=False)
                    mm(dst, h, tl, start=False, stop=False)
                    last = mm(dst, l, th, start=False, stop=True)
                last.then_inc(s["hid_mm"], 1)

            def down(j):
                k, half = divmod(j, 2)
                if half == 0:
                    pe.wait_ge(s["wo_high"], k + 1)
                    pe.wait_ge(*low_of(k, "out"))
                    if k >= 2:
                        pe.wait_ge(s["win_done"], k - 1)
                pe.wait_ge(s["split_high"], j + 1)
                dst = down_bank[k % 2][:, 0:CW]
                for i in range(2):
                    ft = 2 * half + i
                    h, l = (v[:, k % 3, ft * P:(ft + 1) * P] for v in (woh, wol))
                    ah = act_h[:, j % 4, i * CW:(i + 1) * CW]
                    mm(dst, h, ah, start=(ft == 0), stop=False)
                    mm(dst, l, ah, start=False, stop=False)
                pe.wait_ge(s["split_low"], j + 1)
                for i in range(2):
                    ft = 2 * half + i
                    al = act_l[:, j % 4, i * CW:(i + 1) * CW]
                    last = mm(dst, woh[:, k % 3, ft * P:(ft + 1) * P], al, start=False, stop=(ft == FT - 1))
                last.then_inc(s["out_mm"], 1)

            def turn_res(m):
                pe.wait_ge(s["res_fetched"], m + 1)
                if m < 2:
                    pe.wait_ge(s["x_read"], m + 3)
                elif m == 2:
                    pe.wait_ge(s["gelu_done"], 2 * STEPS)
                else:
                    pe.wait_ge(s["total_init"], 1)
                dst = bank[norm1_bank[m]]
                for t in range(TB):
                    last = T.transpose(dst[:, t * P:(t + 1) * P], fetched_res[:, t * P:(t + 1) * P], ident[:])
                last.then_inc(s["res_turned"], 1)

            def turn_y(m):
                pe.wait_ge(s["fetched"], m + 1)
                if isinstance(m, int) and m == 0:
                    pe.wait_ge(s["scaled1"], 1)
                else:
                    pe.wait_ge(s["rmax_done"], m)
                for t in range(TB):
                    last = T.transpose(bank[6][:, t * P:(t + 1) * P], fetched_y[:, t * P:(t + 1) * P], ident[:])
                last.then_inc(s["y_turned"], 1)

            def turn_back(m, norm):
                dst = bank[6 if norm == 2 else norm1_bank[m]]
                pe.wait_ge(s[f"normed{norm}"], m + 1)
                for t in range(TB):
                    last = T.transpose(dst[:, t * P:(t + 1) * P], normal[norm - 1][:, t, :], ident[:])
                last.then_inc(s[f"back{norm}"], 1)

            def route(m):
                pe.wait_ge(s["film_done"], m + 1)
                for t in range(TB):
                    last = mm(bank[6][:, t * E:(t + 1) * E], hf[:, t * P:(t + 1) * P], rw[:], start=True, stop=True)
                last.then_inc(s["logits_mm"], 1)

            def turn_gates(m):
                pe.wait_ge(s["comb_ready"], m + 1)
                pe.wait_ge(s["scaled1"], 2)
                for t in range(TB):
                    last = T.transpose(bank[7][0:E, t * P:(t + 1) * P], comb[:, t, :], ident[:])
                last.then_inc(s["comb_mm"], 1)

            def bias_out(m, first):
                pe.wait_ge(s["comb_copied"], m + 1)
                if first:
                    pe.wait_ge(s["params_late"], 9 * 16)
                    pe.wait_ge(s["scaled1"], NB - 1)
                else:
                    pe.wait_ge(s["scaled1"], NB)
                    pe.wait_ge(s["total_init"], m)
                mm(bank[3][:], b2_r[:], comb_t[:], start=True, stop=True).then_inc(s["bias_mm"], 1)

            def up_v(b, n, fresh=False):
                e, ft = divmod(n, FT)
                if n == 0:
                    pe.wait_ge(s["h_low"], b + 1)
                if fresh:
                    pe.wait_ge(s["v_low"], e + 1)
                    if n < 3:
                        pe.wait_ge(s["gelu_done"], 2 * STEPS)
                before = n - 3 if n >= 3 else max(i for i in range(L) if i % 3 == n) - L
                if not (fresh and n < 3):
                    pe.wait_ge(s["relu_done"], 2 * (L * b + before + 1))
                h, l = (v[:, ft * P:(ft + 1) * P] for v in (vh[:, e, :], vl[e]))
                th, tl = (v[:, bass.ds(b * C, C)] for v in (hh, hl))
                mm(up_bank[n % 3][:], h, th, start=True, stop=False)
                mm(up_bank[n % 3][:], h, tl, start=False, stop=False)
                mm(up_bank[n % 3][:], l, th, start=False, stop=True).then_inc(s["up_mm"], 1)

            def down_v(b, n, fresh):
                e, ft = divmod(n, FT)
                if ft == 0 and not (fresh and e < 2):
                    pe.wait_ge(s["weighted_done"], E * b + e - 1)
                pe.wait_ge(s["relu_done"], 2 * (L * b + n + 1))
                h, l = (v[:, FF + ft * P:FF + (ft + 1) * P] for v in (vh[:, e, :], vl[e]))
                dst, m = down_bank[e % 2][:], n % 4
                mm(dst, h, act_h[:, m, :], start=(ft == 0), stop=False)
                mm(dst, l, act_h[:, m, :], start=False, stop=False)
                pe.wait_ge(s["relu_low"], L * b + n + 1)
                mm(dst, h, act_l[:, m, :], start=False, stop=(ft == FT - 1)).then_inc(s["down_mm"], 1)

            def turn_total(b):
                pe.wait_ge(s["added"], E * (b + 1))
                pe.wait_ge(s["comb_copied"], b + 2)
                for t in range(TB):
                    last = T.transpose(bank[7][:, t * P:(t + 1) * P], total[:, t * P:(t + 1) * P], ident[:])
                last.then_inc(s["out_turned"], 1)

            def experts(b, first, last):
                for n in range(L):
                    if n + LAG < L:
                        up_v(b, n + LAG, first)
                    elif not last:
                        up_v(b + 1, n + LAG - L)
                    down_v(b, n, first)
                    if first and n == 2:
                        turn_gates(b)
                    if n == (9 if first else 3):
                        bias_out(b, first)
                    if n == 6 and not first:
                        turn_total(b - 1)
                    if not last:
                        if n == 1:
                            turn_y(b + 1)
                        if n == (9 if first else 8):
                            turn_back(b + 1, 2)
                        if n == 19:
                            route(b + 1)
                        if n == 30:
                            if not first:
                                pe.wait_ge(s["out_copied"], b)
                            turn_gates(b + 1)
                    if first:
                        if n == 5:
                            turn_back(2, 1)
                        if n == 13:
                            turn_res(NB - 1)
                        if n == 21:
                            turn_back(NB - 1, 1)

            pe.wait_ge(s["starts_ready"], 1)
            words = load_words(pe)
            style(0, emb[:], sorted_subject[:], SE)
            style(1, hw1[:], se_t[:], SH)
            turn_x(0)
            style(2, hw2[:], hyp_t[:], SH)
            style(3, sw1[:], hyp2_t[:], SH2)
            pe.wait_ge(s["pads"], 3)
            up(0)
            pe.wait_ge(s["style_out"], 4)
            mm(bank[7][:, 4 * NS:5 * NS], sw2[:, 0:D], sty_t[:], start=True, stop=True)
            mm(bank[7][:, 5 * NS:6 * NS], sw2[:, D:2 * D], sty_t[:], start=True, stop=True).then_inc(s["style_mm"], 1)

            up(1)
            turn_x(1)
            up(2)
            for j in range(STEPS):
                if j == 0:
                    turn_x(2)
                if j == 4:
                    turn_x(3)
                if j + LAG < STEPS:
                    up(j + LAG)
                down(j)
                if j == 18:
                    turn_res(0)
                if j == 22:
                    turn_back(0, 1)
                if j == 23:
                    turn_res(1)
                if j == 25:
                    turn_y(0)
                if j == 28:
                    turn_back(0, 2)
            turn_res(2)
            route(0)
            up_v(0, 0, True)
            turn_back(1, 1)
            for n in range(1, LAG):
                up_v(0, n, True)
            experts(0, True, False)
            with pe.Fori(1, NB - 1) as b:
                experts(b, False, False)
            experts(NB - 1, False, True)
            pe.wait_ge(s["out_copied"], NB - 1)
            for half in range(2):
                pe.wait_ge(s["last_added"], half + 1)
                for i in range(TB // 2):
                    t = TB // 2 * half + i
                    last = T.transpose(bank[7 - half][:, i * P:(i + 1) * P], total[:, t * P:(t + 1) * P], ident[:])
                last.then_inc(s["last_turned"], 1)


_INS = ['x', 'itok_B_0_7', 'itok_B_6_14', 'L0_cond_Wi', 'L0_cond_bi', 'L0_cond_Wo', 'L0_cond_bo', 'L0_cond_gamma',
        'L0_cond_beta', 'L1_cond_ln_g', 'L1_cond_ln_b', 'L1_cond_subj_emb', 'L1_cond_hyp_w1', 'L1_cond_hyp_b1',
        'L1_cond_hyp_w2', 'L1_cond_hyp_b2', 'L1_cond_sty_w1', 'L1_cond_sty_b1', 'L1_cond_sty_w2', 'L1_cond_sty_b2',
        'L1_cond_router_w', 'L1_cond_exp_w1', 'L1_cond_exp_b1', 'L1_cond_exp_w2', 'L1_cond_exp_b2']


def kernel(**inputs):
    import numpy as _np
    import concourse.bacc as _bacc
    from concourse import mybir as _mybir
    from concourse.bass_utils import run_bass_kernel_spmd as _run

    nc = _bacc.Bacc("TRN2", target_bir_lowering=False, num_devices=1)
    arrays, args = {}, []
    for name in _INS:
        a = _np.ascontiguousarray(inputs[name])
        arrays[f"in_{name}_dram"] = a
        args.append(nc.dram_tensor(f"in_{name}_dram", a.shape, _mybir.dt.from_np(a.dtype), kind="ExternalInput").ap())
    args.append(nc.dram_tensor("out_0_dram", inputs["x"].shape, _mybir.dt.float32, kind="ExternalOutput").ap())
    build(nc, *args)
    r = _run(nc, [arrays], core_ids=[0])
    return r.results[0]["out_0_dram"]
```
